# Optimizing a Trainium2 kernel written in Bass

```python
import numpy as np
import jax
import jax.numpy as jnp

def _softmax(x, axis=-1):
    return jax.nn.softmax(x, axis=axis)
def _gelu(x):
    return jax.nn.gelu(x, approximate=True)
def _silu(x):
    return jax.nn.silu(x)
def _sigmoid(x):
    return jax.nn.sigmoid(x)
def _layernorm(x, axis=-1, eps=1e-5):
    m = jnp.mean(x, axis=axis, keepdims=True)
    v = jnp.var(x, axis=axis, keepdims=True)
    return (x - m) / jnp.sqrt(v + eps)
def _scatter_add(tgt, idx, src, axis=0):
    return tgt.at[idx].add(src)
def _segment_sum(src, seg, n):
    return jax.ops.segment_sum(src, seg, n)

kernel_name = 'mk_conv_preact_d2_conv_nchw64_dcf710'

def setup_inputs(seed: int = 0):
    np.random.seed(seed)
    _w = jnp.asarray
    def _rec_inputs():
        import jax
        import jax.numpy as jnp
        _gk = jax.random.key(seed)
        x = -0.000125 + 0.9999 * jax.random.normal(jax.random.fold_in(_gk, 1), (32, 64, 128, 128), jnp.float32)
        return x
    x = _rec_inputs()
    def _L0_conv_setup():
        import jax, jax.numpy as jnp
        import numpy as np

        def dht_2d(x):
            axes = (2, 3)
            f = jnp.fft.fftn(x, axes=axes)
            ff = jnp.fft.fftn(x[..., ::-1, ::-1], axes=axes)
            result = f.real - ff.imag
            norm = jnp.sqrt(jnp.sum(result * result, axis=axes, keepdims=True))
            safe = jnp.where(norm != 0, norm, 1.0)
            return jnp.where(norm != 0, result / safe, 0.0)

        def idht_2d(X):
            n = X.shape[2] * X.shape[3]
            return dht_2d(X) / n

        def _neg_freq(a):
            return jnp.roll(jnp.flip(a, axis=(-1, -2)), shift=(1, 1), axis=(-1, -2))

        def compl_mul2d(x1, x2):
            x1n = _neg_freq(x1)
            x2n = _neg_freq(x2)
            t1 = jnp.einsum('bixy,ioxy->boxy', x1, x2 + x2n)
            t2 = jnp.einsum('bixy,ioxy->boxy', x1n, x2 - x2n)
            return 0.5 * (t1 + t2)
        key = jax.random.key(seed)
        k1, k2 = jax.random.split(key)
        B, Cin, Cout, H, W, M1, M2 = (32, 64, 64, 128, 128, 20, 20)
        scale = 1.0 / (Cin * Cout)
        x = jax.random.normal(k1, (B, Cin, H, W), dtype=jnp.float32)
        weights1 = scale * jax.random.uniform(k2, (Cin, Cout, M1, M2), dtype=jnp.float32)
        return {'x': x, 'weights1': weights1}
    _L0_conv_all = _L0_conv_setup()
    _L0_conv_in = {k: v for k, v in _L0_conv_all.items() if k in ('weights1', )}
    del _L0_conv_all

    def _L1_conv_setup():
        import jax, jax.numpy as jnp
        import numpy as np
        from jax import lax
        EPS = 1e-08

        def _depthwise_sobel(x):
            c = x.shape[1]
            kx = jnp.array([[-1.0, 0.0, 1.0], [-2.0, 0.0, 2.0], [-1.0, 0.0, 1.0]], dtype=x.dtype)
            ky = jnp.array([[1.0, 2.0, 1.0], [0.0, 0.0, 0.0], [-1.0, -2.0, -1.0]], dtype=x.dtype)
            wx = jnp.tile(kx[None, None], (c, 1, 1, 1))
            wy = jnp.tile(ky[None, None], (c, 1, 1, 1))
            dn = lax.conv_dimension_numbers(x.shape, wx.shape, ('NCHW', 'OIHW', 'NCHW'))
            gx = lax.conv_general_dilated(x, wx, window_strides=(1, 1), padding='SAME', dimension_numbers=dn, feature_group_count=c)
            gy = lax.conv_general_dilated(x, wy, window_strides=(1, 1), padding='SAME', dimension_numbers=dn, feature_group_count=c)
            return jnp.sqrt(gx * gx + gy * gy + EPS)
        key = jax.random.key(seed)
        x = jax.random.normal(key, (16, 64, 256, 256), dtype=jnp.float32)
        return {'x': x}
    _L1_conv_all = _L1_conv_setup()
    _L1_conv_in = {k: v for k, v in _L1_conv_all.items() if k in ()}
    del _L1_conv_all

    return {
        "x": x,
        "L0_conv_weights1": _L0_conv_in["weights1"],
    }

def reference(x, L0_conv_weights1):
    import jax
    import jax.numpy as jnp
    def _L0_conv_ref(x, weights1):
        import jax, jax.numpy as jnp
        import numpy as np

        def dht_2d(x):
            axes = (2, 3)
            f = jnp.fft.fftn(x, axes=axes)
            ff = jnp.fft.fftn(x[..., ::-1, ::-1], axes=axes)
            result = f.real - ff.imag
            norm = jnp.sqrt(jnp.sum(result * result, axis=axes, keepdims=True))
            safe = jnp.where(norm != 0, norm, 1.0)
            return jnp.where(norm != 0, result / safe, 0.0)

        def idht_2d(X):
            n = X.shape[2] * X.shape[3]
            return dht_2d(X) / n

        def _neg_freq(a):
            return jnp.roll(jnp.flip(a, axis=(-1, -2)), shift=(1, 1), axis=(-1, -2))

        def compl_mul2d(x1, x2):
            x1n = _neg_freq(x1)
            x2n = _neg_freq(x2)
            t1 = jnp.einsum('bixy,ioxy->boxy', x1, x2 + x2n)
            t2 = jnp.einsum('bixy,ioxy->boxy', x1n, x2 - x2n)
            return 0.5 * (t1 + t2)
        B, _, H, W = x.shape
        Cout = weights1.shape[1]
        M1, M2 = (weights1.shape[2], weights1.shape[3])
        x_ht = dht_2d(x)
        out_modes = compl_mul2d(x_ht[:, :, :M1, :M2], weights1)
        out_ht = jnp.zeros((B, Cout, H, W), dtype=x.dtype)
        out_ht = out_ht.at[:, :, :M1, :M2].set(out_modes)
        return idht_2d(out_ht)

    def _L1_conv_ref(x):
        import jax, jax.numpy as jnp
        import numpy as np
        from jax import lax
        EPS = 1e-08

        def _depthwise_sobel(x):
            c = x.shape[1]
            kx = jnp.array([[-1.0, 0.0, 1.0], [-2.0, 0.0, 2.0], [-1.0, 0.0, 1.0]], dtype=x.dtype)
            ky = jnp.array([[1.0, 2.0, 1.0], [0.0, 0.0, 0.0], [-1.0, -2.0, -1.0]], dtype=x.dtype)
            wx = jnp.tile(kx[None, None], (c, 1, 1, 1))
            wy = jnp.tile(ky[None, None], (c, 1, 1, 1))
            dn = lax.conv_dimension_numbers(x.shape, wx.shape, ('NCHW', 'OIHW', 'NCHW'))
            gx = lax.conv_general_dilated(x, wx, window_strides=(1, 1), padding='SAME', dimension_numbers=dn, feature_group_count=c)
            gy = lax.conv_general_dilated(x, wy, window_strides=(1, 1), padding='SAME', dimension_numbers=dn, feature_group_count=c)
            return jnp.sqrt(gx * gx + gy * gy + EPS)
        return _depthwise_sobel(x)

    def _gn(v, G=32, eps=1e-5):
        B_, C_, H_, W_ = v.shape
        g = v.reshape(B_, G, C_ // G, H_, W_)
        m = jnp.mean(g, axis=(2, 3, 4), keepdims=True)
        s = jnp.var(g, axis=(2, 3, 4), keepdims=True)
        return ((g - m) / jnp.sqrt(s + eps)).reshape(v.shape)

    def _ln_c(v, eps=1e-6):
        m = jnp.mean(v, axis=1, keepdims=True)
        s = jnp.var(v, axis=1, keepdims=True)
        return (v - m) / jnp.sqrt(s + eps)

    def _ln_t(v, eps=1e-5):
        m = jnp.mean(v, axis=-1, keepdims=True)
        s = jnp.var(v, axis=-1, keepdims=True)
        return (v - m) / jnp.sqrt(s + eps)

    def _to_tokens(v):
        B_, C_, H_, W_ = v.shape
        return v.reshape(B_, C_, H_ * W_).transpose(0, 2, 1)
    def _from_tokens(t, like):
        B_, C_, H_, W_ = like.shape
        return t.transpose(0, 2, 1).reshape(B_, C_, H_, W_)

    x = x + _L0_conv_ref(_gn(x), L0_conv_weights1)
    x = x + _L1_conv_ref(_gn(x))
    return x


_drawn_inputs = setup_inputs


def setup_inputs(seed=0):
    import zlib

    import numpy as np

    out = dict(_drawn_inputs(seed))
    spreads = {}
    factors = {}
    for name, (base, spread) in spreads.items():
        noise = np.random.default_rng([zlib.crc32(name.encode()), seed]).standard_normal(out[name].shape)
        drawn = base * np.exp(spread * noise) if base else spread * noise
        out[name] = jnp.asarray(drawn.astype(out[name].dtype))
    for name, factor in factors.items():
        out[name] = (out[name] * factor).astype(out[name].dtype)
    return out
```

```python
from contextlib import ExitStack

import concourse.bass as bass
import concourse.mybir as mybir
import numpy as np

FP32 = mybir.dt.float32
FP32R = mybir.dt.float32r
ALU = mybir.AluOpType
ACT = mybir.ActivationFunctionType
AX = mybir.AxisListType

B, C, H, W = 32, 64, 128, 128
MODES = 20
NPIX = H * W
PLANES = B * C
TILE = 128
TILES = PLANES // TILE
CHUNK = 16
CHUNKS = TILE // CHUNK
NCHUNK = PLANES // CHUNK
SLOTS = 4
HALF = 8
NB = 2 * MODES + 1
MM = MODES * MODES
SPLIT = 12
OHALF = C // 2
WCH = 8
MGRP = 16
PITCH = 64
TGRP = (NB + 3) // 4
STEPS = TILE // HALF
EPS_NORM = 1e-5
EPS_SOBEL = 1e-8

MATS = ["flip", "flip2_neg", "flip_half", "flip2_neghalf", "smooth", "smooth_neg", "diff", "diff2",
        "ident", "pair", "basis", "ones"]


def load_chunk(eng, buf, x_p, n, sem):
    for h in range(2):
        eng.dma_start(buf[:, HALF * h:HALF * (h + 1), :], x_p[:, bass.ds(n * CHUNK + HALF * h, HALF), :])\
            .then_inc(sem, 16)


def cos_index(j):
    return j


def sin_index(j):
    return MODES + j


def constants():
    n = np.arange(128)
    th = 2 * np.pi / 128
    jj = np.arange(MODES + 1)
    basis = np.concatenate([np.cos(th * np.outer(jj, n)), np.sin(th * np.outer(jj[1:], n))])
    m = {}
    flip = np.zeros((128, 128))
    flip[(-n) % 128, n] = 1
    flip2 = np.zeros((128, 128))
    flip2[(-n - 2) % 128, n] = 1
    m["flip"], m["flip2_neg"], m["flip_half"], m["flip2_neghalf"] = flip, -flip2, flip / 2, -flip2 / 2
    smooth = 2 * np.eye(128) + np.eye(128, k=1) + np.eye(128, k=-1)
    diff = np.eye(128, k=1) - np.eye(128, k=-1)
    m["smooth"], m["smooth_neg"], m["diff"], m["diff2"] = smooth, -smooth, diff, 2 * diff
    m["ident"], m["ones"] = np.eye(128), np.ones((128, 128))
    m["pair"] = np.kron(np.eye(64), np.ones((2, 2)))
    both = np.zeros((128, 128))
    both[0:NB] = basis
    both[64:64 + NB] = basis
    m["basis"] = both
    mats = np.stack([m[k] for k in MATS], 1)

    k2 = np.arange(MODES)
    w = n[:, None]
    second = np.zeros((128, NB, 3, MODES))
    for j in range(MODES + 1):
        late = th * (j + k2[None] * (w + 1))
        c, s = cos_index(j), sin_index(j)
        second[:, c, 0] = -np.sin(th * (k2[None] + 1) * w)
        second[:, c, 1] = np.cos(th * k2[None] * w) - np.sin(late)
        second[:, c, 2] = np.cos(th * k2[None] * w)
        if j:
            second[:, s, 0] = -np.cos(th * (k2[None] + 1) * w)
            second[:, s, 1] = -np.sin(th * k2[None] * w) - np.cos(late)
            second[:, s, 2] = -np.sin(th * k2[None] * w)
    return {"mats": mats.astype(np.float32), "first": basis.T.astype(np.float32).copy(),
            "second": second.reshape(128, NB, 3 * MODES).astype(np.float32)}


def build(nc, x, weights, mats_d, first_d, second_d, out):
    x_p = x.rearrange("b c h w -> h (b c) w")
    out_p = out.rearrange("b c h w -> h (b c) w")
    w_i = weights.rearrange("i o a b -> i o (a b)")

    keep = ExitStack()
    with keep:
        def sb(ctx, name, shape, dt=FP32):
            return ctx.enter_context(nc.sbuf_tensor(name, shape, dt))

        def ps(ctx, name, shape):
            words = int(np.prod(shape[1:]))
            flat = ctx.enter_context(nc.psum_tensor(name, [128, -(-words // 512) * 512], FP32))
            letters = "abcd"[:len(shape) - 1]
            sizes = dict(zip(letters, shape[1:]))
            return flat[:, 0:words].rearrange(f"p ({' '.join(letters)}) -> p {' '.join(letters)}", **sizes)

        def sem(name):
            return keep.enter_context(nc.semaphore(name))

        mats = sb(keep, "mats_sb", [128, len(MATS), 128])
        first = sb(keep, "first_sb", [128, NB])
        xbuf = sb(keep, "xbuf", [128, SLOTS, CHUNK, W])
        modes = sb(keep, "modes", [128, TILES, MM])
        rows = sb(keep, "rows", [128, 2, TILES, TILE])
        mean1 = sb(keep, "mean1", [128, TILES])
        corner = sb(keep, "corner", [128, TILES])

        def mat(name):
            return mats[:, MATS.index(name), :]

        consts_in = sem("consts_in")
        second_in = sem("second_in")
        w_low_in = sem("w_low_in")

        mixing = ExitStack()
        with mixing:
            late = sb(mixing, "late", [128, TILES, MM])
            wmix = sb(mixing, "wmix", [128, OHALF, MM])
            pass1(nc, sb, ps, sem, mat, x_p, w_i, mats, first, xbuf, modes, rows, late, wmix,
                  mats_d, first_d, second_d, consts_in, second_in, w_low_in)
            mix(nc, sb, ps, sem, mat, x_p, w_i, mats, xbuf, modes, rows, late, wmix, mean1, corner,
                w_low_in)
        pass2(nc, sb, ps, sem, mat, x_p, out_p, mats, xbuf, modes, rows, mean1, corner)


def pass1(nc, sb, ps, sem, mat, x_p, w_i, mats, first, xbuf, modes, rows, late, wmix,
          mats_d, first_d, second_d, consts_in, second_in, w_low_in):
    ctx = ExitStack()
    with ctx:
        second = sb(ctx, "second_sb", [128, NB, 3 * MODES])
        tmodes = sb(ctx, "tmodes", [128, NB, TILE])
        prod = sb(ctx, "prod", [128, 2, CHUNK, 68])
        square = sb(ctx, "square", [128, 2, HALF, W])
        t_ps = [ps(ctx, f"t_ps{g}", [128, HALF, NB]) for g in range(2)]
        z_ps = [ps(ctx, f"z_ps{g}", [128, HALF, 64]) for g in range(2)]
        edge_ps = [ps(ctx, f"edge_ps{g}", [128, CHUNK, 2, 2]) for g in range(2)]
        r_ps = [ps(ctx, f"r_ps{g}", [128, 512]) for g in range(2)]

        x_in = [sem(f"p1_x_in{s}") for s in range(SLOTS)]
        pe_first = sem("p1_pe_first")
        pe_mirror = sem("p1_pe_mirror")
        pe_edge = sem("p1_pe_edge")
        pe_second = sem("p1_pe_second")
        first_out = sem("p1_first_out")
        squared = sem("p1_squared")
        modes_out = sem("p1_modes_out")
        mirrored = sem("p1_mirrored")
        edged = sem("p1_edged")
        summed = sem("p1_summed")

        chunk_done = sem("p1_chunk_done")

        block = ctx.enter_context(nc.Block())

        @block.sync
        def _(sp):
            load_chunk(sp, xbuf[:, 0], x_p, 0, x_in[0])
            sp.dma_start(mats[:], mats_d).then_inc(consts_in, 16)
            sp.dma_start(first[:], first_d).then_inc(consts_in, 16)
            for s in range(1, SLOTS):
                load_chunk(sp, xbuf[:, s], x_p, s, x_in[s])
            sp.dma_start(second[:], second_d).then_inc(second_in, 16)
            with sp.Fori(0, NCHUNK // SLOTS - 1) as j:
                for s in range(SLOTS):
                    sp.wait_ge(chunk_done, j * SLOTS + s + 1)
                    load_chunk(sp, xbuf[:, s], x_p, j * SLOTS + s + SLOTS, x_in[s])

        @block.gpsimd
        def _(pool):
            pool.dma_start(wmix[0:C], w_i[:, 0:OHALF, :]).then_inc(w_low_in, 16)

        @block.tensor
        def _(pe):
            pe.wait_ge(consts_in, 32)
            pe.wait_ge(second_in, 16)
            pe.sem_inc(pe_second, 1)
            with pe.Fori(0, TILES) as i:
                for k in range(CHUNKS):
                    slot = k % SLOTS
                    xs = xbuf[:, slot]
                    pe.wait_ge(x_in[slot], (i * 2 + k // SLOTS + 1) * 32)
                    for g in range(2):
                        pe.wait_ge(first_out, i * 16 + 2 * k + g + 1)
                        for p in range(HALF):
                            mm = nc.tensor.matmul(t_ps[g][:, p, :], xs[:, HALF * g + p, :], first[:],
                                                  start=True, stop=True)
                        mm.then_inc(pe_first, 1)
                    for g in range(2):
                        xg = xs[:, HALF * g:HALF * (g + 1), :]
                        pe.wait_ge(mirrored, i * 16 + 2 * k + g + 1)
                        nc.tensor.matmul(z_ps[g][:, :, 1:64], mat("flip"), xg[:, :, 127:64:-1],
                                         start=True, stop=False, skip_group_check=True)
                        nc.tensor.matmul(z_ps[g][:, :, 0:63], mat("flip2_neg"), xg[:, :, 126:63:-1],
                                         start=False, stop=True, skip_group_check=True)\
                            .then_inc(pe_mirror, 1)
                    pe.wait_ge(edged, i * 8 + k + 1)
                    nc.tensor.matmul(edge_ps[k % 2][:, :, 0, :], mat("flip_half"), xs[:, :, 0:65:64],
                                     start=True, stop=True, skip_group_check=True)
                    nc.tensor.matmul(edge_ps[k % 2][:, :, 1, :], mat("flip2_neghalf"), xs[:, :, 63:128:64],
                                     start=False, stop=True, skip_group_check=True).then_inc(pe_edge, 1)
                pe.wait_ge(first_out, i * 16 + 18)
                pe.wait_ge(modes_out, i + 1)
                edge = 2 * SPLIT
                for t in range(NB):
                    j = t if t <= MODES else t - MODES
                    lo, hi = max(2 * j - 1, 0), min(2 * j + 2, 2 * MODES)
                    for bank, (a, b) in enumerate(((lo, min(hi, edge)), (max(lo, edge), hi))):
                        if a >= b:
                            continue
                        skip = a - (2 * j - 1)
                        mm = nc.tensor.matmul(
                            r_ps[bank][:, (a - edge * bank) * MODES:(b - edge * bank) * MODES],
                            tmodes[:, t, :], second[:, t, skip * MODES:(skip + b - a) * MODES],
                            start=t == (0, SPLIT)[bank], stop=t == NB - 1, skip_group_check=True)
                mm.then_inc(pe_second, 1)

        @block.scalar
        def _(act):
            act.sem_inc(first_out, 2)
            act.sem_inc(modes_out, 1)
            with act.Fori(0, TILES) as i:
                act.wait_ge(pe_second, i + 1)
                for k in range(CHUNKS):
                    slot = k % SLOTS
                    for g in range(2):
                        act.wait_ge(pe_first, i * 16 + 2 * k + g + 1)
                        p0 = CHUNK * k + HALF * g
                        nc.scalar.activation(tmodes[:, :, p0:p0 + HALF].rearrange("w t p -> w p t"),
                                             t_ps[g][:], ACT.Copy).then_inc(first_out, 1)
                    act.wait_ge(x_in[slot], (i * 2 + k // SLOTS + 1) * 32)
                    for g in range(2):
                        act.wait_ge(summed, i * 16 + 2 * k + g + 1)
                        nc.scalar.activation(square[:, g], xbuf[:, slot, HALF * g:HALF * (g + 1), :],
                                             ACT.Square).then_inc(squared, 1)
                act.wait_ge(pe_second, i + 2)
                na, nb = SPLIT, MODES - SPLIT
                for dst, which in ((modes, 0), (late, 1)):
                    d = dst[:, bass.ds(i, 1), :].rearrange("p t (a b) -> p (t a) b", b=MODES)
                    ra = r_ps[0][:, 0:na * 2 * MODES].rearrange("p (a v b) -> p a v b", v=2, b=MODES)
                    rb = r_ps[1][:, 0:nb * 2 * MODES].rearrange("p (a v b) -> p a v b", v=2, b=MODES)
                    nc.scalar.activation(d[:, 0:na, :], ra[:, :, which, :], ACT.Copy)
                    last = nc.scalar.activation(d[:, na:, :], rb[:, :, which, :], ACT.Copy)
                last.then_inc(modes_out, 1)

        @block.vector
        def _(dve):
            dve.sem_inc(mirrored, 2)
            dve.sem_inc(edged, 2)
            dve.sem_inc(summed, 2)
            with dve.Fori(0, TILES) as i:
                for k in range(CHUNKS):
                    slot = k % SLOTS
                    xs = xbuf[:, slot]
                    for g in range(2):
                        dve.wait_ge(pe_mirror, i * 16 + 2 * k + g + 1)
                        nc.vector.tensor_tensor(prod[:, k % 2, HALF * g:HALF * (g + 1), 0:64],
                                                xs[:, HALF * g:HALF * (g + 1), 0:64], z_ps[g][:],
                                                ALU.mult).then_inc(mirrored, 1)
                    dve.wait_ge(pe_edge, i * 8 + k + 1)
                    e_x = xs.rearrange("p n (b a) -> p n a b", b=2)
                    for a, col in enumerate((0, 63)):
                        mul = nc.vector.tensor_tensor(prod[:, k % 2, :, 64 + 2 * a:66 + 2 * a],
                                                      e_x[:, :, col, :], edge_ps[k % 2][:, :, a, :], ALU.mult)
                    mul.then_inc(edged, 1)
                    for g in range(2):
                        dve.wait_ge(squared, i * 16 + 2 * k + g + 1)
                        p0 = CHUNK * k + HALF * g
                        nc.vector.tensor_reduce(rows[:, 1, bass.ds(i, 1), p0:p0 + HALF], square[:, g],
                                                axis=AX.X, op=ALU.add).then_inc(summed, 1)
                    dve.wait_ge(mirrored, i * 16 + 2 * k + 4)
                    dve.wait_ge(edged, i * 8 + k + 3)
                    nc.vector.tensor_reduce(rows[:, 0, bass.ds(i, 1), CHUNK * k:CHUNK * (k + 1)],
                                            prod[:, k % 2], axis=AX.X, op=ALU.add).then_inc(chunk_done, 1)


def mirror_pieces(src):
    n = MODES
    return [((slice(0, 1), slice(0, 1)), (slice(0, 1), slice(0, 1))),
            ((slice(0, 1), slice(1, n)), (slice(0, 1), slice(n - 1, 0, -1))),
            ((slice(1, n), slice(0, 1)), (slice(n - 1, 0, -1), slice(0, 1))),
            ((slice(1, n), slice(1, n)), (slice(n - 1, 0, -1), slice(n - 1, 0, -1)))]


def mix(nc, sb, ps, sem, mat, x_p, w_i, mats, xbuf, modes, rows, late, wmix, mean1, corner, w_low_in):
    ctx = ExitStack()
    with ctx:
        xmix = sb(ctx, "xmix", [128, TILES, 2, MM])
        small = sb(ctx, "small", [128, 20, TILES])
        stat_ps = ps(ctx, "stat_ps", [128, 2, TILES])
        pair_ps = ps(ctx, "pair_ps", [128, 2, TILES])
        mix_ps = [ps(ctx, f"mix_ps{g}", [128, MGRP, B]) for g in range(4)]
        wide_ps = [ps(ctx, f"wide_ps{g}", [128, 128]) for g in range(2)]

        stats_pe = sem("m_stats_pe")
        chain = sem("m_chain")
        sums_ready = sem("m_sums_ready")
        paired = sem("m_paired")
        root_in = sem("m_root_in")
        rooted = sem("m_rooted")
        w_low2_in = sem("m_w_low2_in")
        w_raw_in = [sem(f"m_w_raw_in{s}") for s in range(2)]
        w_flipped = sem("m_w_flipped")
        x_mixed = sem("m_x_mixed")
        mixed = sem("m_mixed")
        act_out = sem("m_act_out")
        dve_out = sem("m_dve_out")
        diag_ready = sem("m_diag_ready")
        widened = sem("m_widened")
        wide_out = sem("m_wide_out")

        NW = OHALF // WCH
        GROUPS = MM // MGRP
        raw = xbuf[:].rearrange("p s n w -> p s (n w)")
        block = ctx.enter_context(nc.Block())

        def staged(s):
            return raw[C:128, 2 * s:2 * s + 2, :].rearrange("p s n -> p (s n)")[:, 0:WCH * MM]

        def mixed_pieces(n):
            c, g = divmod(n, GROUPS)
            src = mix_ps[n % 4][OHALF * c:OHALF * (c + 1)].rearrange("o m (t q) -> o q t m", q=2)
            for q in range(2):
                p = C * q + OHALF * c
                yield modes[p:p + OHALF, :, g * MGRP:(g + 1) * MGRP], src[:, q]

        @block.sync
        def _(sp):
            for c in range(2):
                if c == 1:
                    sp.wait_ge(mixed, GROUPS)
                    sp.dma_start(wmix[0:C], w_i[:, OHALF:C, :]).then_inc(w_low2_in, 16)
                for q in range(NW):
                    n = c * NW + q
                    if n >= 2:
                        sp.wait_ge(w_flipped, n - 1)
                    o0 = c * OHALF + q * WCH
                    sp.dma_start(staged(n % 2).rearrange("p (o m) -> p o m", m=MM),
                                 w_i[:, o0:o0 + WCH, :]).then_inc(w_raw_in[n % 2], 16)

        @block.gpsimd
        def _(pool):
            for c in range(2):
                if c == 1:
                    pool.wait_ge(mixed, GROUPS)
                for q in range(NW):
                    n = c * NW + q
                    pool.wait_ge(w_raw_in[n % 2], 16 * (n // 2 + 1))
                    dst = wmix[C:128, q * WCH:(q + 1) * WCH, :].rearrange("p o (a b) -> p o a b", b=MODES)
                    src = staged(n % 2).rearrange("p (o a b) -> p o a b", a=MODES, b=MODES)
                    for d, s in mirror_pieces(None):
                        cp = nc.gpsimd.tensor_copy(dst[:, :, d[0], d[1]], src[:, :, s[0], s[1]])
                    cp.then_inc(w_flipped, 1)

        @block.tensor
        def _(pe):
            for a in range(2):
                for t in range(TILES):
                    mm = nc.tensor.matmul(stat_ps[:, a, t:t + 1], rows[:, a, t, :], mat("ones")[:, 0:1],
                                          start=True, stop=True)
            mm.then_inc(stats_pe, 1)
            pe.wait_ge(sums_ready, 1)
            nc.tensor.matmul(pair_ps[:, 0, :], mat("pair"), small[:, 0, :], start=True, stop=True)\
                .then_inc(paired, 1)
            pe.wait_ge(x_mixed, 1)
            pe.wait_ge(w_low_in, 16)
            for c in range(2):
                if c == 1:
                    pe.wait_ge(w_low2_in, 16)
                pe.wait_ge(w_flipped, (c + 1) * NW)
                for g in range(GROUPS):
                    n = c * GROUPS + g
                    if n >= 4:
                        pe.wait_ge(act_out if n % 2 == 0 else dve_out, n // 2 - 1)
                    for m in range(MGRP):
                        k = g * MGRP + m
                        mm = nc.tensor.matmul(mix_ps[n % 4][OHALF * c:OHALF * (c + 1), m, :],
                                              wmix[:, :, k], xmix[:].rearrange("p t q m -> p (t q) m")[:, :, k],
                                              start=True, stop=True)
                    mm.then_inc(mixed, 1)
            pe.wait_ge(sums_ready, 2)
            nc.tensor.matmul(pair_ps[:].rearrange("p a t -> p (a t)"), mat("pair"),
                             small[:, 8:10, :].rearrange("p a t -> p (a t)"), start=True, stop=True)\
                .then_inc(paired, 1)
            for n in range(2 * TILES):
                pe.wait_ge(diag_ready, n + 1)
                if n >= 2:
                    pe.wait_ge(wide_out, n - 1)
                nc.tensor.matmul(wide_ps[n % 2][:], mat("ones"), xmix[:, n % 2, 0, 0:128],
                                 start=True, stop=True).then_inc(widened, 1)

        @block.scalar
        def _(act):
            act.wait_ge(root_in, 1)
            nc.scalar.activation(small[:, 6, :], small[:, 5, :], ACT.Sqrt, scale=4.0 * NPIX).then_inc(rooted, 1)
            for n in range(0, 2 * GROUPS, 2):
                act.wait_ge(mixed, n + 1)
                for dst, src in mixed_pieces(n):
                    cp = nc.scalar.activation(dst, src, ACT.Copy)
                cp.then_inc(act_out, 1)
            act.wait_ge(root_in, 2)
            nc.scalar.activation(small[:, 6, :], small[:, 5, :], ACT.Sqrt, scale=float(NPIX) ** 3)\
                .then_inc(rooted, 1)
            for n in range(2 * TILES):
                act.wait_ge(widened, n + 1)
                nc.scalar.activation(rows[:, n // TILES, n % TILES, :], wide_ps[n % 2][:], ACT.Copy)\
                    .then_inc(wide_out, 1)

        @block.vector
        def _(dve):
            done = [0]

            def link(ins):
                done[0] += 1
                ins.then_inc(chain, 1)
                dve.wait_ge(chain, done[0])

            V = nc.vector
            s1, diffs, s2, mu, tmp, arg, root, scale = (small[:, n, :] for n in range(8))
            new1, new2, isneg, ms00, m2, xy, var = (small[:, n, :] for n in range(8, 15))

            link(V.tensor_copy(s1, modes[:, :, 0]))
            dve.wait_ge(chain, done[0])
            dve.sem_inc(sums_ready, 1)
            dve.wait_ge(stats_pe, 1)
            link(V.tensor_copy(diffs, stat_ps[:, 0, :]))
            link(V.tensor_copy(s2, stat_ps[:, 1, :]))
            dve.wait_ge(paired, 1)
            link(V.tensor_scalar(mu, pair_ps[:, 0, :], 1.0 / (2 * NPIX), None, ALU.mult))
            link(V.scalar_tensor_tensor(modes[:, :, 0], mu, -float(NPIX), s1, ALU.mult, ALU.add))
            link(V.tensor_tensor(tmp, modes[:, :, 0], s1, ALU.subtract))
            link(V.tensor_tensor(arg, s1, modes[:, :, 0], ALU.add))
            link(V.tensor_tensor(arg, arg, mu, ALU.mult))
            link(V.tensor_tensor(arg, s2, arg, ALU.subtract))
            link(V.tensor_tensor(arg, arg, diffs, ALU.add))

            def inverse_root(n, extra):
                link(V.tensor_scalar(isneg, arg, 0.0, None, ALU.is_le))
                V.tensor_tensor(arg, arg, isneg, ALU.max).then_inc(root_in, 1)
                dve.wait_ge(rooted, n)
                link(V.reciprocal(scale, root))
                link(V.tensor_scalar(isneg, isneg, -1.0, 1.0, ALU.mult, ALU.add))
                link(V.tensor_tensor(scale, scale, isneg, ALU.mult))

            inverse_root(1, None)
            link(V.tensor_tensor(modes[:], modes[:], scale.unsqueeze(2).to_broadcast([128, TILES, MM]), ALU.mult))
            for q in range(2):
                part = slice(C * q, C * (q + 1))
                src = modes[part].rearrange("p t (a b) -> p t a b", b=MODES)
                for op, dpart in ((ALU.add, slice(0, C)), (ALU.subtract, slice(C, 128))):
                    dst = xmix[dpart, :, q, :].rearrange("p t (a b) -> p t a b", b=MODES)
                    for d, s in mirror_pieces(None):
                        for t0 in ((0,) if True else ()):
                            last = V.tensor_tensor(dst[:, :, d[0], d[1]], src[:, :, d[0], d[1]],
                                                   src[:, :, s[0], s[1]], op)
                        link(last)
            dve.sem_inc(x_mixed, 1)

            for n in range(1, 2 * GROUPS, 2):
                dve.wait_ge(mixed, n + 1)
                for dst, src in mixed_pieces(n):
                    cp = V.tensor_copy(dst, src)
                cp.then_inc(dve_out, 1)
            dve.wait_ge(dve_out, GROUPS)
            dve.wait_ge(act_out, GROUPS)
            scratch = xmix[:].rearrange("p t q m -> p (t q m)")[:, 0:TILES * MM].rearrange("p (t m) -> p t m", m=MM)
            link(V.tensor_tensor(scratch, modes[:], modes[:], ALU.mult))
            link(V.tensor_reduce(m2, scratch, axis=AX.X, op=ALU.add))
            link(V.scalar_tensor_tensor(arg, scratch[:, :, 0], 0.5, m2, ALU.mult, ALU.add))
            link(V.tensor_copy(m2, arg))
            inverse_root(2, None)
            link(V.tensor_tensor(modes[:], modes[:], scale.unsqueeze(2).to_broadcast([128, TILES, MM]), ALU.mult))
            link(V.tensor_copy(ms00, modes[:, :, 0]))
            link(V.tensor_tensor(scratch, modes[:], late[:], ALU.mult))
            link(V.tensor_reduce(xy, scratch, axis=AX.X, op=ALU.add))
            link(V.scalar_tensor_tensor(new1, ms00, float(NPIX), s1, ALU.mult, ALU.add))
            link(V.tensor_tensor(m2, m2, scale, ALU.mult))
            link(V.tensor_tensor(m2, m2, scale, ALU.mult))
            link(V.scalar_tensor_tensor(new2, xy, 2.0, s2, ALU.mult, ALU.add))
            link(V.scalar_tensor_tensor(new2, m2, float(NPIX), new2, ALU.mult, ALU.add))
            dve.sem_inc(sums_ready, 1)
            dve.wait_ge(paired, 2)
            link(V.tensor_scalar(mean1[:], pair_ps[:, 0, :], 1.0 / (2 * NPIX), None, ALU.mult))
            link(V.tensor_tensor(tmp, mean1[:], mean1[:], ALU.mult))
            link(V.scalar_tensor_tensor(var, pair_ps[:, 1, :], 1.0 / (2 * NPIX), tmp, ALU.mult, ALU.subtract))
            link(V.tensor_scalar(var, var, 0.0, EPS_NORM, ALU.max, ALU.add))
            link(V.reciprocal(var, var))
            link(V.tensor_tensor(corner[:], ms00, mean1[:], ALU.subtract))
            for n in range(2 * TILES):
                value = (var if n < TILES else mean1[:])[:, n % TILES:n % TILES + 1]
                if n >= 2:
                    dve.wait_ge(widened, n - 1)
                V.tensor_scalar(xmix[:, n % 2, 0, 0:128], mat("ident"), value, None, ALU.mult)\
                    .then_inc(diag_ready, 1)


def pass2(nc, sb, ps, sem, mat, x_p, out_p, mats, xbuf, modes, rows, mean1, corner):
    ctx = ExitStack()
    with ctx:
        coef_flat = sb(ctx, "coef", [128, NB * NB + 128])
        coef = coef_flat[:, 0:NB * NB].rearrange("p (a b) -> p a b", b=NB)
        staged = sb(ctx, "staged", [128, MM])
        coef_t = sb(ctx, "coef_t", [NB, 2, TILE, PITCH])
        v_sb = sb(ctx, "v_sb", [128, 2, HALF // 2, W])
        x_hi = sb(ctx, "x_hi", [128, 2, HALF, W + 2], FP32R)
        x_lo = sb(ctx, "x_lo", [128, 2, HALF, W + 2], FP32R)
        stencil = sb(ctx, "stencil", [128, 4, 128], FP32R)
        grad = sb(ctx, "grad", [128, 2, 2, 2, 512])
        eps = sb(ctx, "eps", [128, 1])
        v_ps = ps(ctx, "v_ps", [128, HALF // 2, W])
        t_ps = ps(ctx, "t_ps", [128, 4, TILE])
        y_ps = ps(ctx, "y_ps", [128, 2, HALF // 2, W])
        g_ps = [ps(ctx, f"g_ps{h}", [128, 2, 4, W]) for h in range(2)]

        x_in = [sem(f"p2_x_in{s}") for s in range(SLOTS)]
        stored = [sem(f"p2_stored{s}") for s in range(SLOTS)]
        setup = sem("p2_setup")
        cleared = sem("p2_cleared")
        coef_staged = sem("p2_coef_staged")
        coef_main = sem("p2_coef_main")
        coef_ready = sem("p2_coef_ready")
        pe_t = sem("p2_pe_t")
        coef_out = sem("p2_coef_out")
        pe_v = sem("p2_pe_v")
        v_out = sem("p2_v_out")
        pe_y = sem("p2_pe_y")
        centred = sem("p2_centred")
        hi_ready = sem("p2_hi_ready")
        lo_ready = sem("p2_lo_ready")
        pe_grad = sem("p2_pe_grad")
        squared = sem("p2_squared")
        added = sem("p2_added")
        rooted = sem("p2_rooted")
        finished = sem("p2_finished")

        PERIOD = 2 * STEPS
        ALL = TILES * STEPS
        block = ctx.enter_context(nc.Block())

        def over_steps(eng, step):
            step(0, 0)
            with eng.Fori(0, ALL // PERIOD - 1) as i:
                for r in range(1, PERIOD + 1):
                    step(i, r)
            for r in range(1, PERIOD):
                step(ALL // PERIOD - 1, r)

        def x_of(r):
            c, h = divmod(r, 2)
            return xbuf[:, c % SLOTS, HALF * h:HALF * (h + 1), :]

        def at(i, r):
            return i * PERIOD + r

        def before(i, r, n):
            return isinstance(i, int) and at(i, r) < n

        def beyond(i, r):
            return isinstance(i, int) and at(i, r) >= ALL

        def tile_of(i, r):
            return i * (PERIOD // STEPS) + r // STEPS

        def first_plane(i, r):
            return at(i, r) * HALF

        @block.sync
        def _(sp):
            for s in range(SLOTS):
                load_chunk(sp, xbuf[:, s], x_p, s, x_in[s])

            def store(n0, c):
                done = sp.snap((n0 + c) * 2 + 3)
                plane = sp.snap((n0 + c) * CHUNK)
                sp.wait_ge(finished, done)
                sp.dma_start(out_p[:, bass.ds(plane, CHUNK), :], xbuf[:, c % SLOTS])\
                    .then_inc(stored[c % SLOTS], 16)

            store(0, 0)
            with sp.Fori(0, NCHUNK // SLOTS - 1) as j:
                for c in range(1, SLOTS + 1):
                    store(j * SLOTS, c)
                    s = (c - 1) % SLOTS
                    count = sp.snap((j + 1) * 16)
                    chunk = sp.snap(j * SLOTS + c + SLOTS - 1)
                    sp.wait_ge(stored[s], count)
                    load_chunk(sp, xbuf[:, s], x_p, chunk, x_in[s])
            for c in range(1, SLOTS):
                store(NCHUNK - SLOTS, c)
            for s in range(SLOTS):
                sp.wait_ge(stored[s], NCHUNK // SLOTS * 16)

        @block.gpsimd
        def _(pool):
            n = MODES
            nc.gpsimd.memset(coef_flat[:], 0.0).then_inc(cleared, 1)
            nc.gpsimd.memset(coef_t[:, :, :, NB:PITCH], 0.0).then_inc(cleared, 1)
            pool.wait_ge(cleared, 2)

            def coefficients(t):
                nc.gpsimd.tensor_copy(staged[:], modes[:, bass.ds(t, 1), :].rearrange("p t m -> p (t m)"))\
                    .then_inc(coef_staged, 1)
                pool.wait_ge(coef_staged, t + 1)
                m = staged[:].rearrange("p (a b) -> p a b", b=n)
                c0, c1, s1 = slice(0, n), slice(1, n + 1), slice(n + 1, 2 * n + 1)
                nc.gpsimd.tensor_copy(coef[:, c0, c0], m)
                nc.gpsimd.tensor_scalar(coef[:, n + 1:2 * n, n + 1:2 * n], m[:, 1:, 1:], -1.0, None, ALU.mult)
                nc.gpsimd.tensor_scalar(coef[:, s1, c1], m, -1.0, None, ALU.mult)
                nc.gpsimd.tensor_scalar(coef[:, c1, s1], m, -1.0, None, ALU.mult).then_inc(coef_main, 1)
                pool.wait_ge(coef_main, t + 1)
                nc.gpsimd.tensor_copy(coef[:, 0, 0:1], corner[:, bass.ds(t, 1)]).then_inc(coef_ready, 1)

            coefficients(0)
            for t in range(1, TILES):
                pool.wait_ge(pe_t, t * TGRP)
                coefficients(t)

        @block.tensor
        def _(pe):
            def transposes(t, par, g):
                if g == 0:
                    pe.wait_ge(coef_ready, t + 1)
                pe.wait_ge(coef_out, t * TGRP + g)
                for j in range(4 * g, min(4 * g + 4, NB)):
                    mm = nc.tensor.transpose(t_ps[:, j - 4 * g, :], coef_flat[:, NB * j:NB * j + 128], mat("ident"))
                mm.then_inc(pe_t, 1)

            def second_axis(i, r):
                if r % STEPS == 0:
                    pe.wait_ge(coef_out, (tile_of(i, r) + 1) * TGRP)
                if not before(i, r, 1):
                    pe.wait_ge(v_out, at(i, r))
                p0 = (r % STEPS) * HALF
                for q in range(HALF // 2):
                    mm = nc.tensor.matmul(
                        v_ps[:, q, :],
                        coef_t[0:NB, r // STEPS % 2, p0 + 2 * q:p0 + 2 * q + 2, :].rearrange("k p j -> k (p j)"),
                        mat("basis")[0:NB, :], start=True, stop=True)
                mm.then_inc(pe_v, 1)

            def first_axis(i, r):
                pe.wait_ge(v_out, at(i, r) + 1)
                if not before(i, r, 1):
                    pe.wait_ge(centred, at(i, r))
                for q in range(2):
                    mm = nc.tensor.matmul(y_ps[:, q], mat("basis")[64 * q:64 * q + NB, :],
                                          v_sb[64 * q:64 * q + NB, r % 2], start=True, stop=True)
                mm.then_inc(pe_y, 1)

            def sobel(i, r):
                pe.wait_ge(lo_ready, at(i, r) + 1)
                SM, SMN, D, D2 = range(4)
                taps = [(0, SMN, 0), (0, SM, 2), (1, D, 0), (1, D2, 1), (1, D, 2)]
                for h in range(2):
                    if not before(i, r, 1):
                        pe.wait_ge(squared, at(i, r) * 2 + h - 1)
                    for axis in range(2):
                        todo = [(x, m, o) for a, m, o in taps if a == axis for x in (x_hi, x_lo)]
                        for n, (x, m, o) in enumerate(todo):
                            mm = nc.tensor.matmul(g_ps[h][:, axis], stencil[:, m, :],
                                                  x[:, r % 2, 4 * h:4 * h + 4, o:o + W],
                                                  start=n == 0, stop=n == len(todo) - 1)
                    mm.then_inc(pe_grad, 1)

            for g in range(TGRP):
                transposes(0, 0, g)
            second_axis(0, 0)
            second_axis(0, 1)
            pe.wait_ge(setup, 1)
            first_axis(0, 0)

            def step(i, r):
                s = r % STEPS
                if not beyond(i, r + 2):
                    second_axis(i, r + 2)
                if 2 <= s < 2 + TGRP and not beyond(i, r - s + STEPS):
                    transposes(tile_of(i, r) + 1, (r // STEPS + 1) % 2, s - 2)
                if not beyond(i, r + 1):
                    first_axis(i, r + 1)
                sobel(i, r)

            over_steps(pe, step)

        @block.scalar
        def _(act):
            def high(i, r):
                act.wait_ge(centred, at(i, r) + 1)
                if not before(i, r, 2):
                    act.wait_ge(pe_grad, at(i, r) * 2 - 2)
                nc.scalar.activation(x_hi[:, r % 2, :, 1:W + 1], x_of(r), ACT.Copy).then_inc(hi_ready, 1)

            def copy_v(i, r):
                act.wait_ge(pe_v, at(i, r) + 1)
                if not before(i, r, 2):
                    act.wait_ge(pe_y, at(i, r) - 1)
                nc.scalar.activation(v_sb[:, r % 2], v_ps[:], ACT.Copy).then_inc(v_out, 1)

            def squares(i, r, h):
                act.wait_ge(pe_grad, at(i, r) * 2 + h + 1)
                if not before(i, r, 2):
                    act.wait_ge(finished, at(i, r))
                nc.scalar.activation(grad[:, r % 2, h], g_ps[h][:].rearrange("p a n w -> p a (n w)"),
                                     ACT.Square).then_inc(squared, 1)

            def roots(i, r, h):
                act.wait_ge(added, at(i, r) * 2 + h + 1)
                inv_var = rows[:, 0].rearrange("p t n -> p (t n)")
                for k in range(2):
                    f = grad[:, r % 2, h, 0, 256 * k:256 * (k + 1)]
                    a = nc.scalar.activation(f, f, ACT.Sqrt, bias=eps[:],
                                             scale=inv_var[:, bass.ds(first_plane(i, r) + 4 * h + 2 * k, 1)])
                a.then_inc(rooted, 1)

            act.wait_ge(setup, 1)
            copy_v(0, 0)
            copy_v(0, 1)
            high(0, 0)

            def step(i, r):
                if not before(i, r, 1):
                    roots(i, r - 1, 0)
                    roots(i, r - 1, 1)
                if not beyond(i, r + 1):
                    high(i, r + 1)
                if not beyond(i, r + 2):
                    copy_v(i, r + 2)
                squares(i, r, 0)
                squares(i, r, 1)

            over_steps(act, step)
            roots(ALL // PERIOD - 1, PERIOD - 1, 0)
            roots(ALL // PERIOD - 1, PERIOD - 1, 1)

        @block.vector
        def _(dve):
            V = nc.vector
            dve.sem_inc(finished, 1)
            for n, m in enumerate(("smooth", "smooth_neg", "diff", "diff2")):
                V.tensor_copy(stencil[:, n, :], mat(m))
            for buf in (x_hi, x_lo):
                V.memset(buf[:, :, :, 0:1].bitcast(FP32), 0.0)
                V.memset(buf[:, :, :, W + 1:W + 2].bitcast(FP32), 0.0)
            V.memset(eps[:], EPS_SOBEL).then_inc(setup, 1)

            def copy_coef(t, par, g):
                n = min(4, NB - 4 * g)
                dve.wait_ge(pe_t, t * TGRP + g + 1)
                V.tensor_copy(coef_t[:, par, :, 4 * g:4 * g + n].rearrange("k p j -> k j p"),
                              t_ps[0:NB, 0:n, :]).then_inc(coef_out, 1)

            def centre(i, r):
                dve.wait_ge(pe_y, at(i, r) + 1)
                c = r // 2
                dve.wait_ge(x_in[c % SLOTS], (i * (PERIOD // 2 // SLOTS) + c // SLOTS + 1) * 32)
                xs = x_of(r).rearrange("p (k q) w -> p q k w", q=2)
                V.tensor_tensor(xs, xs, y_ps[:], ALU.add).then_inc(centred, 1)

            def low(i, r):
                dve.wait_ge(hi_ready, at(i, r) + 1)
                if not before(i, r, 2):
                    dve.wait_ge(pe_grad, at(i, r) * 2 - 2)
                V.tensor_tensor(x_lo[:, r % 2, :, 1:W + 1], x_of(r), x_hi[:, r % 2, :, 1:W + 1].bitcast(FP32),
                                ALU.subtract).then_inc(lo_ready, 1)

            def add(i, r, h):
                dve.wait_ge(squared, at(i, r) * 2 + h + 1)
                f = grad[:, r % 2, h]
                V.tensor_tensor(f[:, 0], f[:, 0], f[:, 1], ALU.add).then_inc(added, 1)

            def finish(i, r):
                mean = rows[:, 1].rearrange("p t n -> p (t n)")
                for h in range(2):
                    dve.wait_ge(rooted, at(i, r) * 2 + h + 1)
                    for k in range(2):
                        xs = x_of(r)[:, 4 * h + 2 * k:4 * h + 2 * k + 2, :].rearrange("p n w -> p (n w)")
                        v = V.scalar_tensor_tensor(
                            xs, xs, mean[:, bass.ds(first_plane(i, r) + 4 * h + 2 * k, 1)],
                            grad[:, r % 2, h, 0, 256 * k:256 * (k + 1)], ALU.add, ALU.add)
                v.then_inc(finished, 1)

            dve.wait_ge(cleared, 2)
            for g in range(TGRP):
                copy_coef(0, 0, g)
            centre(0, 0)
            low(0, 0)

            def step(i, r):
                s = r % STEPS
                if not beyond(i, r + 1):
                    centre(i, r + 1)
                if not before(i, r, 1):
                    finish(i, r - 1)
                if 2 <= s < 2 + TGRP and not beyond(i, r - s + STEPS):
                    copy_coef(tile_of(i, r) + 1, (r // STEPS + 1) % 2, s - 2)
                if not beyond(i, r + 1):
                    low(i, r + 1)
                add(i, r, 0)
                add(i, r, 1)

            over_steps(dve, step)
            finish(ALL // PERIOD - 1, PERIOD - 1)


def kernel(x, L0_conv_weights1):
    import concourse.bacc as bacc
    from concourse.bass_utils import run_bass_kernel_spmd

    nc = bacc.Bacc("TRN2", target_bir_lowering=False, num_devices=1)
    arrays = {"x": np.ascontiguousarray(x), "weights": np.ascontiguousarray(L0_conv_weights1), **constants()}
    aps = {k: nc.dram_tensor(k, v.shape, mybir.dt.from_np(v.dtype), kind="ExternalInput").ap()
           for k, v in arrays.items()}
    out = nc.dram_tensor("out", (B, C, H, W), FP32, kind="ExternalOutput").ap()
    build(nc, aps["x"], aps["weights"], aps["mats"], aps["first"], aps["second"], out)
    r = run_bass_kernel_spmd(nc, [arrays], core_ids=[0])
    return r.results[0]["out"]
```

```python
from contextlib import ExitStack

import concourse.bass as bass
import concourse.mybir as mybir
import numpy as np

FP32 = mybir.dt.float32
FP32R = mybir.dt.float32r
ALU = mybir.AluOpType
ACT = mybir.ActivationFunctionType
AX = mybir.AxisListType

B, C, H, W = 32, 64, 128, 128
MODES = 20
NPIX = H * W
PLANES = B * C
TILE = 128
TILES = PLANES // TILE
CHUNK = 16
CHUNKS = TILE // CHUNK
NCHUNK = PLANES // CHUNK
SLOTS = 4
HALF = 8
NB = 2 * MODES + 1
MM = MODES * MODES
SPLIT = 12
OHALF = C // 2
WCH = 8
MGRP = 16
PITCH = 64
TGRP = (NB + 3) // 4
STEPS = TILE // HALF
XSTEPS = SLOTS * CHUNK // HALF
EPS_NORM = 1e-5
EPS_SOBEL = 1e-8

MATS = ["flip", "flip2_neg", "flip_half", "flip2_neghalf", "smooth", "smooth_neg", "diff",
        "ident", "pair", "basis", "ones"]


def load_chunk(eng, buf, x_p, n, sem):
    for h in range(2):
        eng.dma_start(buf[:, HALF * h:HALF * (h + 1), :], x_p[:, bass.ds(n * CHUNK + HALF * h, HALF), :])\
            .then_inc(sem, 16)


def cos_index(j):
    return j


def sin_index(j):
    return MODES + j


def constants():
    n = np.arange(128)
    th = 2 * np.pi / 128
    jj = np.arange(MODES + 1)
    basis = np.concatenate([np.cos(th * np.outer(jj, n)), np.sin(th * np.outer(jj[1:], n))])
    m = {}
    flip = np.zeros((128, 128))
    flip[(-n) % 128, n] = 1
    flip2 = np.zeros((128, 128))
    flip2[(-n - 2) % 128, n] = 1
    m["flip"], m["flip2_neg"], m["flip_half"], m["flip2_neghalf"] = flip, -flip2, flip / 2, -flip2 / 2
    smooth = 2 * np.eye(128) + np.eye(128, k=1) + np.eye(128, k=-1)
    diff = np.eye(128, k=1) - np.eye(128, k=-1)
    m["smooth"], m["smooth_neg"], m["diff"] = smooth, -smooth, diff
    m["ident"], m["ones"] = np.eye(128), np.ones((128, 128))
    m["pair"] = np.kron(np.eye(64), np.ones((2, 2)))
    both = np.zeros((128, 128))
    both[0:NB] = basis
    both[64:64 + NB] = basis
    m["basis"] = both
    mats = np.stack([m[k] for k in MATS], 1)

    k2 = np.arange(MODES)
    w = n[:, None]
    second = np.zeros((128, NB, 3, MODES))
    for j in range(MODES + 1):
        late = th * (j + k2[None] * (w + 1))
        c, s = cos_index(j), sin_index(j)
        second[:, c, 0] = -np.sin(th * (k2[None] + 1) * w)
        second[:, c, 1] = np.cos(th * k2[None] * w) - np.sin(late)
        second[:, c, 2] = np.cos(th * k2[None] * w)
        if j:
            second[:, s, 0] = -np.cos(th * (k2[None] + 1) * w)
            second[:, s, 1] = -np.sin(th * k2[None] * w) - np.cos(late)
            second[:, s, 2] = -np.sin(th * k2[None] * w)
    return {"mats": mats.astype(np.float32), "first": np.pad(basis.T, ((0, 0), (0, PITCH - NB))).astype(np.float32),
            "second": second.reshape(128, NB, 3 * MODES).astype(np.float32)}


def build(nc, x, weights, mats_d, first_d, second_d, out):
    x_p = x.rearrange("b c h w -> h (b c) w")
    out_p = out.rearrange("b c h w -> h (b c) w")
    w_i = weights.rearrange("i o a b -> i o (a b)")

    keep = ExitStack()
    with keep:
        def sb(ctx, name, shape, dt=FP32):
            return ctx.enter_context(nc.sbuf_tensor(name, shape, dt))

        def ps(ctx, name, shape):
            words = int(np.prod(shape[1:]))
            flat = ctx.enter_context(nc.psum_tensor(name, [128, -(-words // 512) * 512], FP32))
            letters = "abcd"[:len(shape) - 1]
            sizes = dict(zip(letters, shape[1:]))
            return flat[:, 0:words].rearrange(f"p ({' '.join(letters)}) -> p {' '.join(letters)}", **sizes)

        def sem(name):
            return keep.enter_context(nc.semaphore(name))

        mats = sb(keep, "mats_sb", [128, len(MATS), 128])
        first = sb(keep, "first_sb", [128, PITCH])
        xbuf = sb(keep, "xbuf", [128, SLOTS, CHUNK, W])
        modes = sb(keep, "modes", [128, TILES, MM])
        rows = sb(keep, "rows", [128, 2, TILES, TILE])
        mean1 = sb(keep, "mean1", [128, TILES])
        corner = sb(keep, "corner", [128, TILES])

        def mat(name):
            return mats[:, MATS.index(name), :]

        mixing = ExitStack()
        with mixing:
            late = sb(mixing, "late", [128, TILES, MM])
            pass1(nc, sb, ps, sem, mat, x_p, mats, first, xbuf, modes, rows, late, mats_d, first_d, second_d)
            mix(nc, sb, ps, sem, mat, w_i, xbuf, modes, rows, late, mean1, corner)
        pass2(nc, sb, ps, sem, mat, x_p, out_p, mats, xbuf, modes, rows, mean1, corner)


def pass1(nc, sb, ps, sem, mat, x_p, mats, first, xbuf, modes, rows, late, mats_d, first_d, second_d):
    ctx = ExitStack()
    with ctx:
        second = sb(ctx, "second_sb", [128, NB, 3 * MODES])
        tmodes = sb(ctx, "tmodes", [128, 2, NB, TILE])
        x_hi = sb(ctx, "m_hi", [128, 2, HALF, 64], FP32R)
        x_lo = sb(ctx, "m_lo", [128, 2, HALF, 64], FP32R)
        flips = sb(ctx, "flips", [128, 2, 128], FP32R)
        prod = sb(ctx, "prod", [128, 2, CHUNK, 68])
        square = sb(ctx, "square", [128, 2, HALF, W])
        t_ps = [ps(ctx, f"t_ps{g}", [128, HALF, PITCH]) for g in range(2)]
        z_ps = [ps(ctx, f"z_ps{g}", [128, 64, HALF]) for g in range(2)]
        edge_ps = [ps(ctx, f"edge_ps{g}", [128, CHUNK, 2, 2]) for g in range(2)]
        r_ps = [ps(ctx, f"r_ps{g}", [128, 512]) for g in range(2)]

        consts_in = sem("consts_in")
        second_in = sem("second_in")
        x_in = [sem(f"p1_x_in{s}") for s in range(SLOTS)]
        flips_ready = sem("p1_flips_ready")
        pe_first = sem("p1_pe_first")
        pe_mirror = sem("p1_pe_mirror")
        pe_edge = sem("p1_pe_edge")
        pe_second = sem("p1_pe_second")
        first_out = sem("p1_first_out")
        hi_ready = sem("p1_hi_ready")
        lo_ready = sem("p1_lo_ready")
        squared = sem("p1_squared")
        modes_out = sem("p1_modes_out")
        mirrored = sem("p1_mirrored")
        edged = sem("p1_edged")
        summed = sem("p1_summed")
        chunk_done = sem("p1_chunk_done")

        HALVES = 2 * CHUNKS
        block = ctx.enter_context(nc.Block())

        def over_tiles(eng, tile):
            tile(0, 0)
            with eng.Fori(0, TILES // 2 - 1) as j:
                tile(j * 2 + 1, 1)
                tile(j * 2 + 2, 0)
            tile(TILES - 1, 1)

        def is_first(i):
            return isinstance(i, int) and i == 0

        def arrived(i, k):
            return (i * (CHUNKS // SLOTS) + k // SLOTS + 1) * 32

        @block.sync
        def _(sp):
            load_chunk(sp, xbuf[:, 0], x_p, 0, x_in[0])
            sp.dma_start(mats[:], mats_d).then_inc(consts_in, 16)
            sp.dma_start(first[:], first_d).then_inc(consts_in, 16)
            for s in range(1, SLOTS):
                load_chunk(sp, xbuf[:, s], x_p, s, x_in[s])
            sp.dma_start(second[:], second_d).then_inc(second_in, 16)
            with sp.Fori(0, NCHUNK // SLOTS - 1) as j:
                for s in range(SLOTS):
                    sp.wait_ge(chunk_done, j * SLOTS + s + 1)
                    load_chunk(sp, xbuf[:, s], x_p, j * SLOTS + s + SLOTS, x_in[s])

        @block.gpsimd
        def _(pool):
            def tile(i, par):
                for k in range(CHUNKS):
                    for g in range(2):
                        pool.wait_ge(hi_ready, i * HALVES + 2 * k + g + 1)
                        nc.gpsimd.tensor_tensor(x_lo[:, g], xbuf[:, k % SLOTS, HALF * g:HALF * (g + 1), 64:],
                                                x_hi[:, g].bitcast(FP32), ALU.subtract).then_inc(lo_ready, 1)

            over_tiles(pool, tile)

        @block.tensor
        def _(pe):
            pe.wait_ge(consts_in, 32)
            pe.wait_ge(second_in, 16)
            pe.wait_ge(flips_ready, 2)
            pe.sem_inc(pe_second, 2)
            pe.sem_inc(pe_mirror, 2)

            per_chunk = -(-NB // (CHUNKS - 1))

            def second_axis(i, par, k):
                if k == 0:
                    pe.wait_ge(first_out, (i + 1) * HALVES + 2)
                    pe.wait_ge(modes_out, i + 1)
                edge = 2 * SPLIT
                for t in range(per_chunk * k, min(per_chunk * (k + 1), NB)):
                    j = t if t <= MODES else t - MODES
                    lo, hi = max(2 * j - 1, 0), min(2 * j + 2, 2 * MODES)
                    for bank, (a, b) in enumerate(((lo, min(hi, edge)), (max(lo, edge), hi))):
                        if a >= b:
                            continue
                        skip = a - (2 * j - 1)
                        mm = nc.tensor.matmul(
                            r_ps[bank][:, (a - edge * bank) * MODES:(b - edge * bank) * MODES],
                            tmodes[:, par, t, :], second[:, t, skip * MODES:(skip + b - a) * MODES],
                            start=t == (0, SPLIT)[bank], stop=t == NB - 1, skip_group_check=True)
                if k == CHUNKS - 2:
                    mm.then_inc(pe_second, 1)

            def tile(i, par):
                for k in range(CHUNKS):
                    slot = k % SLOTS
                    xs = xbuf[:, slot]
                    pe.wait_ge(x_in[slot], arrived(i, k))
                    for g in range(2):
                        pe.wait_ge(first_out, i * HALVES + 2 * k + g + 1)
                        for p in range(HALF):
                            mm = nc.tensor.matmul(t_ps[g][:, p, :], xs[:, HALF * g + p, :], first[:],
                                                  start=True, stop=True)
                        mm.then_inc(pe_first, 1)
                        if g and not is_first(i) and k < CHUNKS - 1:
                            second_axis(i - 1, 1 - par, k)
                        pe.wait_ge(mirrored, i * HALVES + 2 * k + g + 1)
                        pe.wait_ge(lo_ready, i * HALVES + 2 * k + g + 1)
                        for n, part in enumerate((x_hi, x_lo)):
                            rev = part[:, g, :, ::-1].rearrange("p n w -> p w n")
                            nc.tensor.matmul(z_ps[g][:, 1:64, :], flips[:, 0, :], rev[:, 0:63, :],
                                             start=n == 0, stop=False, skip_group_check=True)
                            mm = nc.tensor.matmul(z_ps[g][:, 0:63, :], flips[:, 1, :], rev[:, 1:64, :],
                                                  start=False, stop=n == 1, skip_group_check=True)
                        mm.then_inc(pe_mirror, 1)
                    pe.wait_ge(edged, i * CHUNKS + k + 1)
                    nc.tensor.matmul(edge_ps[k % 2][:, :, 0, :], mat("flip_half"), xs[:, :, 0:65:64],
                                     start=True, stop=True, skip_group_check=True)
                    nc.tensor.matmul(edge_ps[k % 2][:, :, 1, :], mat("flip2_neghalf"), xs[:, :, 63:128:64],
                                     start=False, stop=True, skip_group_check=True).then_inc(pe_edge, 1)

            over_tiles(pe, tile)
            for k in range(CHUNKS - 1):
                second_axis(TILES - 1, 1, k)

        @block.scalar
        def _(act):
            act.sem_inc(first_out, 2)
            act.sem_inc(modes_out, 1)

            def high(i, k, g):
                act.wait_ge(x_in[k % SLOTS], arrived(i, k))
                act.wait_ge(pe_mirror, i * HALVES + 2 * k + g + 1)
                nc.scalar.activation(x_hi[:, g], xbuf[:, k % SLOTS, HALF * g:HALF * (g + 1), 64:],
                                     ACT.Copy).then_inc(hi_ready, 1)

            def copy_modes(i):
                act.wait_ge(pe_second, i + 3)
                na, nb = SPLIT, MODES - SPLIT
                for dst, which in ((modes, 0), (late, 1)):
                    d = dst[:, bass.ds(i, 1), :].rearrange("p t (a b) -> p (t a) b", b=MODES)
                    ra = r_ps[0][:, 0:na * 2 * MODES].rearrange("p (a v b) -> p a v b", v=2, b=MODES)
                    rb = r_ps[1][:, 0:nb * 2 * MODES].rearrange("p (a v b) -> p a v b", v=2, b=MODES)
                    nc.scalar.activation(d[:, 0:na, :], ra[:, :, which, :], ACT.Copy)
                    last = nc.scalar.activation(d[:, na:, :], rb[:, :, which, :], ACT.Copy)
                last.then_inc(modes_out, 1)

            def tile(i, par):
                act.wait_ge(pe_second, i + 1)
                for k in range(CHUNKS):
                    for g in range(2):
                        high(i, k, g)
                        act.wait_ge(summed, i * HALVES + 2 * k + g + 1)
                        nc.scalar.activation(square[:, g], xbuf[:, k % SLOTS, HALF * g:HALF * (g + 1), :],
                                             ACT.Square).then_inc(squared, 1)
                        act.wait_ge(pe_first, i * HALVES + 2 * k + g + 1)
                        p0 = CHUNK * k + HALF * g
                        nc.scalar.activation(tmodes[:, par, :, p0:p0 + HALF].rearrange("w t p -> w p t"),
                                             t_ps[g][:, :, 0:NB], ACT.Copy).then_inc(first_out, 1)
                if not is_first(i):
                    copy_modes(i - 1)

            over_tiles(act, tile)
            copy_modes(TILES - 1)

        @block.vector
        def _(dve):
            dve.sem_inc(mirrored, 2)
            dve.sem_inc(edged, 2)
            dve.sem_inc(summed, 2)
            dve.wait_ge(consts_in, 32)
            nc.vector.tensor_copy(flips[:, 0, :], mat("flip")).then_inc(flips_ready, 1)
            nc.vector.tensor_copy(flips[:, 1, :], mat("flip2_neg")).then_inc(flips_ready, 1)

            def tile(i, par):
                for k in range(CHUNKS):
                    slot = k % SLOTS
                    xs = xbuf[:, slot]
                    for g in range(2):
                        dve.wait_ge(squared, i * HALVES + 2 * k + g + 1)
                        p0 = CHUNK * k + HALF * g
                        nc.vector.tensor_reduce(rows[:, 1, bass.ds(i, 1), p0:p0 + HALF], square[:, g],
                                                axis=AX.X, op=ALU.add).then_inc(summed, 1)
                    for g in range(2):
                        dve.wait_ge(pe_mirror, i * HALVES + 2 * k + g + 3)
                        nc.vector.tensor_tensor(prod[:, k % 2, HALF * g:HALF * (g + 1), 0:64],
                                                xs[:, HALF * g:HALF * (g + 1), 0:64],
                                                z_ps[g].rearrange("p w n -> p n w"),
                                                ALU.mult).then_inc(mirrored, 1)
                    dve.wait_ge(pe_edge, i * CHUNKS + k + 1)
                    e_x = xs.rearrange("p n (b a) -> p n a b", b=2)
                    for a, col in enumerate((0, 63)):
                        mul = nc.vector.tensor_tensor(prod[:, k % 2, :, 64 + 2 * a:66 + 2 * a],
                                                      e_x[:, :, col, :], edge_ps[k % 2][:, :, a, :], ALU.mult)
                    mul.then_inc(edged, 1)
                    dve.wait_ge(mirrored, i * HALVES + 2 * k + 4)
                    dve.wait_ge(edged, i * CHUNKS + k + 3)
                    nc.vector.tensor_reduce(rows[:, 0, bass.ds(i, 1), CHUNK * k:CHUNK * (k + 1)],
                                            prod[:, k % 2], axis=AX.X, op=ALU.add).then_inc(chunk_done, 1)

            over_tiles(dve, tile)


def mirror_pieces():
    n = MODES
    return [((slice(0, 1), slice(0, 1)), (slice(0, 1), slice(0, 1))),
            ((slice(0, 1), slice(1, n)), (slice(0, 1), slice(n - 1, 0, -1))),
            ((slice(1, n), slice(0, 1)), (slice(n - 1, 0, -1), slice(0, 1))),
            ((slice(1, n), slice(1, n)), (slice(n - 1, 0, -1), slice(n - 1, 0, -1)))]


def mix(nc, sb, ps, sem, mat, w_i, xbuf, modes, rows, late, mean1, corner):
    ctx = ExitStack()
    with ctx:
        xmix = sb(ctx, "xmix", [128, TILES, 2, MM])
        wmix = sb(ctx, "wmix", [128, OHALF, MM])
        small = sb(ctx, "small", [128, 20, TILES])
        stat_ps = ps(ctx, "stat_ps", [128, 2, TILES])
        pair_ps = ps(ctx, "pair_ps", [128, 2, TILES])
        mix_ps = [ps(ctx, f"mix_ps{g}", [128, MGRP, B]) for g in range(4)]
        wide_ps = [ps(ctx, f"wide_ps{g}", [128, 128]) for g in range(2)]

        stats_pe = sem("m_stats_pe")
        chain = sem("m_chain")
        sums_ready = sem("m_sums_ready")
        paired = sem("m_paired")
        root_in = sem("m_root_in")
        rooted = sem("m_rooted")
        w_low_in = sem("m_w_low_in")
        w_raw_in = [sem(f"m_w_raw_in{s}") for s in range(2)]
        w_flipped = sem("m_w_flipped")
        parted = sem("m_parted")
        moved_up = sem("m_moved_up")
        moved_down = sem("m_moved_down")
        x_mixed = sem("m_x_mixed")
        mixed = sem("m_mixed")
        act_out = sem("m_act_out")
        dve_out = sem("m_dve_out")
        diag_ready = sem("m_diag_ready")
        widened = sem("m_widened")
        wide_out = sem("m_wide_out")

        NW = OHALF // WCH
        GROUPS = MM // MGRP
        raw = xbuf[:].rearrange("p s n w -> p s (n w)")
        block = ctx.enter_context(nc.Block())

        def staged(s):
            return raw[C:128, 2 * s:2 * s + 2, :].rearrange("p s n -> p (s n)")[:, 0:WCH * MM]

        def mixed_pieces(n):
            c, g = divmod(n, GROUPS)
            src = mix_ps[n % 4][OHALF * c:OHALF * (c + 1)].rearrange("o m (t q) -> o q t m", q=2)
            for q in range(2):
                p = C * q + OHALF * c
                yield modes[p:p + OHALF, :, g * MGRP:(g + 1) * MGRP], src[:, q]

        @block.sync
        def _(sp):
            for c in range(2):
                if c == 1:
                    sp.wait_ge(mixed, GROUPS)
                for q in range(NW):
                    n = c * NW + q
                    if n >= 2:
                        sp.wait_ge(w_flipped, n - 1)
                    o0 = c * OHALF + q * WCH
                    sp.dma_start(staged(n % 2).rearrange("p (o m) -> p o m", m=MM),
                                 w_i[:, o0:o0 + WCH, :]).then_inc(w_raw_in[n % 2], 16)
                    sp.dma_start(wmix[0:C, q * WCH:(q + 1) * WCH], w_i[:, o0:o0 + WCH, :])\
                        .then_inc(w_low_in, 16)

        @block.tensor
        def _(pe):
            for a in range(2):
                for t in range(TILES):
                    mm = nc.tensor.matmul(stat_ps[:, a, t:t + 1], rows[:, a, t, :], mat("ones")[:, 0:1],
                                          start=True, stop=True)
            mm.then_inc(stats_pe, 1)
            pe.wait_ge(sums_ready, 1)
            nc.tensor.matmul(pair_ps[:, 0, :], mat("pair"), small[:, 0, :], start=True, stop=True)\
                .then_inc(paired, 1)
            pe.wait_ge(x_mixed, 1)
            for c in range(2):
                pe.wait_ge(w_low_in, (c + 1) * NW * 16)
                pe.wait_ge(w_flipped, (c + 1) * NW)
                for g in range(GROUPS):
                    n = c * GROUPS + g
                    if n >= 4:
                        pe.wait_ge(act_out if n % 2 == 0 else dve_out, n // 2 - 1)
                    for m in range(MGRP):
                        k = g * MGRP + m
                        mm = nc.tensor.matmul(mix_ps[n % 4][OHALF * c:OHALF * (c + 1), m, :],
                                              wmix[:, :, k], xmix[:].rearrange("p t q m -> p (t q) m")[:, :, k],
                                              start=True, stop=True)
                    mm.then_inc(mixed, 1)
            pe.wait_ge(sums_ready, 2)
            nc.tensor.matmul(pair_ps[:].rearrange("p a t -> p (a t)"), mat("pair"),
                             small[:, 8:10, :].rearrange("p a t -> p (a t)"), start=True, stop=True)\
                .then_inc(paired, 1)
            for n in range(2 * TILES):
                pe.wait_ge(diag_ready, n + 1)
                if n >= 2:
                    pe.wait_ge(wide_out, n - 1)
                nc.tensor.matmul(wide_ps[n % 2][:], mat("ones"), xmix[:, n % 2, 0, 0:128],
                                 start=True, stop=True).then_inc(widened, 1)

        @block.scalar
        def _(act):
            def mirror_weights(n):
                act.wait_ge(w_raw_in[n % 2], 16 * (n // 2 + 1))
                q = n % NW
                dst = wmix[C:128, q * WCH:(q + 1) * WCH, :].rearrange("p o (a b) -> p o a b", b=MODES)
                src = staged(n % 2).rearrange("p (o a b) -> p o a b", a=MODES, b=MODES)
                for d, s in mirror_pieces():
                    cp = nc.scalar.activation(dst[:, :, d[0], d[1]], src[:, :, s[0], s[1]], ACT.Copy)
                cp.then_inc(w_flipped, 1)

            act.wait_ge(root_in, 1)
            nc.scalar.activation(small[:, 6, :], small[:, 5, :], ACT.Sqrt, scale=4.0 * NPIX).then_inc(rooted, 1)
            for n in range(NW):
                mirror_weights(n)
            act.wait_ge(parted, 1)
            nc.scalar.activation(modes[0:C], xmix[C:128, :, 0, :], ACT.Copy).then_inc(moved_up, 1)
            act.wait_ge(moved_down, 1)
            act.wait_ge(moved_up, 1)
            nc.scalar.activation(xmix[0:C, :, 1, :], modes[0:C], ACT.Copy).then_inc(x_mixed, 1)
            for n in range(0, 2 * GROUPS, 2):
                if n == GROUPS + 1:
                    act.wait_ge(mixed, GROUPS)
                    for piece in range(NW, 2 * NW):
                        mirror_weights(piece)
                act.wait_ge(mixed, n + 1)
                for dst, src in mixed_pieces(n):
                    cp = nc.scalar.activation(dst, src, ACT.Copy)
                cp.then_inc(act_out, 1)
            act.wait_ge(root_in, 2)
            nc.scalar.activation(small[:, 6, :], small[:, 5, :], ACT.Sqrt, scale=float(NPIX) ** 3)\
                .then_inc(rooted, 1)
            for n in range(2 * TILES):
                act.wait_ge(widened, n + 1)
                nc.scalar.activation(rows[:, n // TILES, n % TILES, :], wide_ps[n % 2][:], ACT.Copy)\
                    .then_inc(wide_out, 1)

        @block.vector
        def _(dve):
            done = [0]

            def link(ins):
                done[0] += 1
                ins.then_inc(chain, 1)
                dve.wait_ge(chain, done[0])

            V = nc.vector
            s1, diffs, s2, mu, tmp, arg, root, scale = (small[:, n, :] for n in range(8))
            new1, new2, isneg, ms00, m2, xy, var = (small[:, n, :] for n in range(8, 15))

            link(V.tensor_copy(s1, modes[:, :, 0]))
            dve.wait_ge(chain, done[0])
            dve.sem_inc(sums_ready, 1)
            dve.wait_ge(stats_pe, 1)
            link(V.tensor_copy(diffs, stat_ps[:, 0, :]))
            link(V.tensor_copy(s2, stat_ps[:, 1, :]))
            dve.wait_ge(paired, 1)
            link(V.tensor_scalar(mu, pair_ps[:, 0, :], 1.0 / (2 * NPIX), None, ALU.mult))
            link(V.scalar_tensor_tensor(modes[:, :, 0], mu, -float(NPIX), s1, ALU.mult, ALU.add))
            link(V.tensor_tensor(tmp, modes[:, :, 0], s1, ALU.subtract))
            link(V.tensor_tensor(arg, s1, modes[:, :, 0], ALU.add))
            link(V.tensor_tensor(arg, arg, mu, ALU.mult))
            link(V.tensor_tensor(arg, s2, arg, ALU.subtract))
            link(V.tensor_tensor(arg, arg, diffs, ALU.add))

            def inverse_root(n, extra):
                link(V.tensor_scalar(isneg, arg, 0.0, None, ALU.is_le))
                V.tensor_tensor(arg, arg, isneg, ALU.max).then_inc(root_in, 1)
                dve.wait_ge(rooted, n)
                link(V.reciprocal(scale, root))
                link(V.tensor_scalar(isneg, isneg, -1.0, 1.0, ALU.mult, ALU.add))
                link(V.tensor_tensor(scale, scale, isneg, ALU.mult))

            inverse_root(1, None)
            link(V.tensor_tensor(modes[:], modes[:], scale.unsqueeze(2).to_broadcast([128, TILES, MM]), ALU.mult))
            src = modes[:].rearrange("p t (a b) -> p t a b", b=MODES)
            for q, op in enumerate((ALU.add, ALU.subtract)):
                dst = xmix[:, :, q, :].rearrange("p t (a b) -> p t a b", b=MODES)
                for d, s in mirror_pieces():
                    last = V.tensor_tensor(dst[:, :, d[0], d[1]], src[:, :, d[0], d[1]],
                                           src[:, :, s[0], s[1]], op)
            last.then_inc(parted, 1)
            dve.wait_ge(parted, 1)
            dve.wait_ge(moved_up, 1)
            V.tensor_copy(xmix[C:128, :, 0, :], xmix[0:C, :, 1, :]).then_inc(moved_down, 1)

            for n in range(1, 2 * GROUPS, 2):
                dve.wait_ge(mixed, n + 1)
                for dst, src in mixed_pieces(n):
                    cp = V.tensor_copy(dst, src)
                cp.then_inc(dve_out, 1)
            dve.wait_ge(dve_out, GROUPS)
            dve.wait_ge(act_out, GROUPS)
            scratch = xmix[:].rearrange("p t q m -> p (t q m)")[:, 0:TILES * MM].rearrange("p (t m) -> p t m", m=MM)
            link(V.tensor_tensor(scratch, modes[:], modes[:], ALU.mult))
            link(V.tensor_reduce(m2, scratch, axis=AX.X, op=ALU.add))
            link(V.scalar_tensor_tensor(arg, scratch[:, :, 0], 0.5, m2, ALU.mult, ALU.add))
            link(V.tensor_copy(m2, arg))
            inverse_root(2, None)
            link(V.tensor_tensor(modes[:], modes[:], scale.unsqueeze(2).to_broadcast([128, TILES, MM]), ALU.mult))
            link(V.tensor_copy(ms00, modes[:, :, 0]))
            link(V.tensor_tensor(scratch, modes[:], late[:], ALU.mult))
            link(V.tensor_reduce(xy, scratch, axis=AX.X, op=ALU.add))
            link(V.scalar_tensor_tensor(new1, ms00, float(NPIX), s1, ALU.mult, ALU.add))
            link(V.tensor_tensor(m2, m2, scale, ALU.mult))
            link(V.tensor_tensor(m2, m2, scale, ALU.mult))
            link(V.scalar_tensor_tensor(new2, xy, 2.0, s2, ALU.mult, ALU.add))
            link(V.scalar_tensor_tensor(new2, m2, float(NPIX), new2, ALU.mult, ALU.add))
            dve.sem_inc(sums_ready, 1)
            dve.wait_ge(paired, 2)
            link(V.tensor_scalar(mean1[:], pair_ps[:, 0, :], 1.0 / (2 * NPIX), None, ALU.mult))
            link(V.tensor_tensor(tmp, mean1[:], mean1[:], ALU.mult))
            link(V.scalar_tensor_tensor(var, pair_ps[:, 1, :], 1.0 / (2 * NPIX), tmp, ALU.mult, ALU.subtract))
            link(V.tensor_scalar(var, var, 0.0, EPS_NORM, ALU.max, ALU.add))
            link(V.reciprocal(var, var))
            link(V.tensor_tensor(corner[:], ms00, mean1[:], ALU.subtract))
            for n in range(2 * TILES):
                value = (var if n < TILES else mean1[:])[:, n % TILES:n % TILES + 1]
                if n >= 2:
                    dve.wait_ge(widened, n - 1)
                V.tensor_scalar(xmix[:, n % 2, 0, 0:128], mat("ident"), value, None, ALU.mult)\
                    .then_inc(diag_ready, 1)


def pass2(nc, sb, ps, sem, mat, x_p, out_p, mats, xbuf, modes, rows, mean1, corner):
    ctx = ExitStack()
    with ctx:
        coef_flat = sb(ctx, "coef", [128, NB * NB + 128])
        coef = coef_flat[:, 0:NB * NB].rearrange("p (a b) -> p a b", b=NB)
        coef_t = sb(ctx, "coef_t", [NB, 2, TILE, PITCH])
        v_sb = sb(ctx, "v_sb", [128, 2, 2, HALF // 2, W], FP32R)
        basis = sb(ctx, "basis", [128, 2, 128], FP32R)
        pairs = sb(ctx, "pairs", [128, 2, HALF, W + 2])
        p_hi = sb(ctx, "p_hi", [128, 2, HALF, W + 2], FP32R)
        p_lo = sb(ctx, "p_lo", [128, 2, HALF, W + 2], FP32R)
        stencil = sb(ctx, "stencil", [128, 3, 128], FP32R)
        grad = sb(ctx, "grad", [128, 2, 2, 2, 512])
        eps = sb(ctx, "eps", [128, 1])
        v_ps = ps(ctx, "v_ps", [128, HALF // 2, W])
        t_ps = ps(ctx, "t_ps", [128, 4, TILE])
        y_ps = ps(ctx, "y_ps", [128, 2, HALF // 2, W])
        g_ps = [ps(ctx, f"g_ps{h}", [128, 2, 4, W]) for h in range(2)]

        x_in = [sem(f"p2_x_in{s}") for s in range(XSTEPS)]
        stored = [sem(f"p2_stored{s}") for s in range(XSTEPS)]
        setup = sem("p2_setup")
        cleared = sem("p2_cleared")
        basis_hi = sem("p2_basis_hi")
        coef_main = sem("p2_coef_main")
        coef_ready = sem("p2_coef_ready")
        pe_t = sem("p2_pe_t")
        coef_out = sem("p2_coef_out")
        pe_v = sem("p2_pe_v")
        v_hi = sem("p2_v_hi")
        v_out = sem("p2_v_out")
        pe_y = sem("p2_pe_y")
        centred = sem("p2_centred")
        pairs_ready = sem("p2_pairs_ready")
        hi_ready = sem("p2_hi_ready")
        lo_ready = sem("p2_lo_ready")
        pe_grad = sem("p2_pe_grad")
        squared = sem("p2_squared")
        added = sem("p2_added")
        rooted = sem("p2_rooted")
        finished = sem("p2_finished")

        PERIOD = 2 * STEPS
        ALL = TILES * STEPS
        block = ctx.enter_context(nc.Block())

        def over_steps(eng, step):
            step(0, 0)
            with eng.Fori(0, ALL // PERIOD - 1) as i:
                for r in range(1, PERIOD + 1):
                    step(i, r)
            for r in range(1, PERIOD):
                step(ALL // PERIOD - 1, r)

        def x_of(r):
            c, h = divmod(r, 2)
            return xbuf[:, c % SLOTS, HALF * h:HALF * (h + 1), :]

        def at(i, r):
            return i * PERIOD + r

        def before(i, r, n):
            return isinstance(i, int) and at(i, r) < n

        def beyond(i, r):
            return isinstance(i, int) and at(i, r) >= ALL

        def tile_of(i, r):
            return i * (PERIOD // STEPS) + r // STEPS

        def first_plane(i, r):
            return at(i, r) * HALF

        @block.sync
        def _(sp):
            def load(u, slot):
                sp.dma_start(x_of(slot), x_p[:, bass.ds(u * HALF, HALF), :]).then_inc(x_in[slot], 16)

            def store(u0, slot):
                done = sp.snap(u0 + slot + 2)
                plane = sp.snap((u0 + slot) * HALF)
                sp.wait_ge(finished, done)
                sp.dma_start(out_p[:, bass.ds(plane, HALF), :], x_of(slot)).then_inc(stored[slot], 16)

            for slot in range(XSTEPS):
                load(slot, slot)
            with sp.Fori(0, ALL // XSTEPS - 1) as j:
                for slot in range(XSTEPS):
                    store(j * XSTEPS, slot)
                    count = sp.snap((j + 1) * 16)
                    after = sp.snap((j + 1) * XSTEPS + slot)
                    sp.wait_ge(stored[slot], count)
                    load(after, slot)
            for slot in range(XSTEPS):
                store(ALL - XSTEPS, slot)
            for slot in range(XSTEPS):
                sp.wait_ge(stored[slot], ALL // XSTEPS * 16)

        @block.gpsimd
        def _(pool):
            nc.gpsimd.memset(coef_flat[:], 0.0).then_inc(cleared, 1)
            nc.gpsimd.memset(coef_t[:, :, :, NB:PITCH], 0.0).then_inc(cleared, 1)
            nc.gpsimd.memset(v_sb[:].bitcast(FP32), 0.0).then_inc(cleared, 1)

            def neighbours(i, r):
                pool.wait_ge(centred, at(i, r) + 1)
                if not before(i, r, 2):
                    pool.wait_ge(lo_ready, at(i, r) - 1)
                u, q = x_of(r), pairs[:, r % 2]
                nc.gpsimd.tensor_tensor(q[:, :, 1:W], u[:, :, 0:W - 1], u[:, :, 1:W], ALU.add)
                nc.gpsimd.tensor_copy(q[:, :, 0:W + 1:W], u[:, :, 0:W:W - 1]).then_inc(pairs_ready, 1)

            def add(i, r):
                for h in range(2):
                    pool.wait_ge(squared, at(i, r) * 2 + h + 1)
                    f = grad[:, r % 2, h]
                    nc.gpsimd.tensor_tensor(f[:, 0], f[:, 0], f[:, 1], ALU.add).then_inc(added, 1)

            def step(i, r):
                if not before(i, r, 1):
                    add(i, r - 1)
                if not beyond(i, r + 2):
                    neighbours(i, r + 2)

            neighbours(0, 0)
            neighbours(0, 1)
            over_steps(pool, step)
            add(ALL // PERIOD - 1, PERIOD - 1)

        @block.tensor
        def _(pe):
            def transposes(t, par, g):
                if g == 0:
                    pe.wait_ge(coef_ready, t + 1)
                pe.wait_ge(coef_out, t * TGRP + g)
                for j in range(4 * g, min(4 * g + 4, NB)):
                    mm = nc.tensor.transpose(t_ps[:, j - 4 * g, :], coef_flat[:, NB * j:NB * j + 128], mat("ident"))
                mm.then_inc(pe_t, 1)

            def second_axis(i, r):
                if r % STEPS == 0:
                    pe.wait_ge(coef_out, (tile_of(i, r) + 1) * TGRP)
                if not before(i, r, 1):
                    pe.wait_ge(v_out, at(i, r))
                p0 = (r % STEPS) * HALF
                for q in range(HALF // 2):
                    mm = nc.tensor.matmul(
                        v_ps[:, q, :],
                        coef_t[0:NB, r // STEPS % 2, p0 + 2 * q:p0 + 2 * q + 2, :].rearrange("k p j -> k (p j)"),
                        mat("basis")[0:NB, :], start=True, stop=True)
                mm.then_inc(pe_v, 1)

            def first_axis(i, r):
                pe.wait_ge(v_out, at(i, r) + 1)
                if not before(i, r, 1):
                    pe.wait_ge(centred, at(i, r))
                for q in range(2):
                    for n in range(2):
                        mm = nc.tensor.matmul(y_ps[:, q], basis[:, n, :], v_sb[:, r % 2, q],
                                              start=n == 0, stop=n == 1)
                mm.then_inc(pe_y, 1)

            def sobel(i, r):
                pe.wait_ge(lo_ready, at(i, r) + 1)
                SMOOTH, SMOOTH_NEG, DIFF = range(3)
                taps = [(0, SMOOTH_NEG, 0), (0, SMOOTH, 1), (1, DIFF, 0), (1, DIFF, 1)]
                for h in range(2):
                    if not before(i, r, 1):
                        pe.wait_ge(squared, at(i, r) * 2 + h - 1)
                    for axis in range(2):
                        todo = [(x, m, o) for a, m, o in taps if a == axis for x in (p_hi, p_lo)]
                        for n, (x, m, o) in enumerate(todo):
                            mm = nc.tensor.matmul(g_ps[h][:, axis], stencil[:, m, :],
                                                  x[:, r % 2, 4 * h:4 * h + 4, o:o + W],
                                                  start=n == 0, stop=n == len(todo) - 1)
                    mm.then_inc(pe_grad, 1)

            for g in range(TGRP):
                transposes(0, 0, g)
            second_axis(0, 0)
            second_axis(0, 1)
            pe.wait_ge(setup, 1)
            first_axis(0, 0)
            for u in range(2, 4):
                second_axis(0, u)
                first_axis(0, u - 1)

            def step(i, r):
                s = r % STEPS
                if not beyond(i, r + 4):
                    second_axis(i, r + 4)
                if not beyond(i, r + 3):
                    first_axis(i, r + 3)
                if 1 <= s < 1 + TGRP and not beyond(i, r - s + STEPS):
                    transposes(tile_of(i, r) + 1, (r // STEPS + 1) % 2, s - 1)
                sobel(i, r)

            over_steps(pe, step)

        @block.scalar
        def _(act):
            def high(i, r):
                act.wait_ge(pairs_ready, at(i, r) + 1)
                if not before(i, r, 2):
                    act.wait_ge(pe_grad, at(i, r) * 2 - 2)
                nc.scalar.activation(p_hi[:, r % 2, :, 0:W + 1], pairs[:, r % 2, :, 0:W + 1], ACT.Copy)\
                    .then_inc(hi_ready, 1)

            def copy_v(i, r):
                act.wait_ge(pe_v, at(i, r) + 1)
                if not before(i, r, 2):
                    act.wait_ge(pe_y, at(i, r) - 1)
                for q in range(2):
                    v = nc.scalar.activation(v_sb[0:NB, r % 2, q], v_ps[64 * q:64 * q + NB], ACT.Copy)
                v.then_inc(v_hi, 1)

            def squares(i, r, h):
                act.wait_ge(pe_grad, at(i, r) * 2 + h + 1)
                if not before(i, r, 2):
                    act.wait_ge(finished, at(i, r))
                nc.scalar.activation(grad[:, r % 2, h], g_ps[h][:].rearrange("p a n w -> p a (n w)"),
                                     ACT.Square).then_inc(squared, 1)

            def roots(i, r, h):
                act.wait_ge(added, at(i, r) * 2 + h + 1)
                inv_var = rows[:, 0].rearrange("p t n -> p (t n)")
                for k in range(2):
                    f = grad[:, r % 2, h, 0, 256 * k:256 * (k + 1)]
                    a = nc.scalar.activation(f, f, ACT.Sqrt, bias=eps[:],
                                             scale=inv_var[:, bass.ds(first_plane(i, r) + 4 * h + 2 * k, 1)])
                a.then_inc(rooted, 1)

            act.wait_ge(setup, 1)
            act.wait_ge(cleared, 3)
            for u in range(4):
                copy_v(0, u)
            high(0, 0)

            def step(i, r):
                if not beyond(i, r + 4):
                    copy_v(i, r + 4)
                if not before(i, r, 1):
                    roots(i, r - 1, 0)
                if not beyond(i, r + 1):
                    high(i, r + 1)
                if not before(i, r, 1):
                    roots(i, r - 1, 1)
                squares(i, r, 0)
                squares(i, r, 1)

            over_steps(act, step)
            roots(ALL // PERIOD - 1, PERIOD - 1, 0)
            roots(ALL // PERIOD - 1, PERIOD - 1, 1)

        @block.vector
        def _(dve):
            V = nc.vector
            dve.sem_inc(finished, 1)
            for n, m in enumerate(("smooth", "smooth_neg", "diff")):
                V.tensor_copy(stencil[:, n, :], mat(m))
            V.tensor_copy(basis[:, 0, :], mat("basis")).then_inc(basis_hi, 1)
            dve.wait_ge(basis_hi, 1)
            V.tensor_tensor(basis[:, 1, :], mat("basis"), basis[:, 0, :].bitcast(FP32), ALU.subtract)
            V.memset(eps[:], EPS_SOBEL).then_inc(setup, 1)

            def copy_coef(t, par, g):
                n = min(4, NB - 4 * g)
                dve.wait_ge(pe_t, t * TGRP + g + 1)
                V.tensor_copy(coef_t[:, par, :, 4 * g:4 * g + n].rearrange("k p j -> k j p"),
                              t_ps[0:NB, 0:n, :]).then_inc(coef_out, 1)

            def centre(i, r):
                dve.wait_ge(pe_y, at(i, r) + 1)
                dve.wait_ge(x_in[r % XSTEPS], (i * (PERIOD // XSTEPS) + r // XSTEPS + 1) * 16)
                xs = x_of(r).rearrange("p (k q) w -> p q k w", q=2)
                V.tensor_tensor(xs, xs, y_ps[:], ALU.add).then_inc(centred, 1)

            def low(i, r):
                dve.wait_ge(hi_ready, at(i, r) + 1)
                if not before(i, r, 2):
                    dve.wait_ge(pe_grad, at(i, r) * 2 - 2)
                V.tensor_tensor(p_lo[:, r % 2, :, 0:W + 1], pairs[:, r % 2, :, 0:W + 1],
                                p_hi[:, r % 2, :, 0:W + 1].bitcast(FP32), ALU.subtract).then_inc(lo_ready, 1)

            def low_v(i, r):
                dve.wait_ge(v_hi, at(i, r) + 1)
                for q in range(2):
                    v = V.tensor_tensor(v_sb[64:64 + NB, r % 2, q], v_ps[64 * q:64 * q + NB],
                                        v_sb[0:NB, r % 2, q].bitcast(FP32), ALU.subtract)
                v.then_inc(v_out, 1)

            def coefficients(t):
                n = MODES
                m = modes[:, bass.ds(t, 1), :].rearrange("p t (a b) -> p (t a) b", b=n)
                c0, c1, s1 = slice(0, n), slice(1, n + 1), slice(n + 1, 2 * n + 1)
                V.tensor_copy(coef[:, c0, c0], m)
                V.tensor_scalar(coef[:, n + 1:2 * n, n + 1:2 * n], m[:, 1:, 1:], -1.0, None, ALU.mult)
                V.tensor_scalar(coef[:, s1, c1], m, -1.0, None, ALU.mult)
                V.tensor_scalar(coef[:, c1, s1], m, -1.0, None, ALU.mult).then_inc(coef_main, 1)
                dve.wait_ge(coef_main, t + 1)
                V.tensor_copy(coef[:, 0, 0:1], corner[:, bass.ds(t, 1)]).then_inc(coef_ready, 1)

            def finish(i, r):
                mean = rows[:, 1].rearrange("p t n -> p (t n)")
                for h in range(2):
                    dve.wait_ge(rooted, at(i, r) * 2 + h + 1)
                    for k in range(2):
                        xs = x_of(r)[:, 4 * h + 2 * k:4 * h + 2 * k + 2, :].rearrange("p n w -> p (n w)")
                        v = V.scalar_tensor_tensor(
                            xs, xs, mean[:, bass.ds(first_plane(i, r) + 4 * h + 2 * k, 1)],
                            grad[:, r % 2, h, 0, 256 * k:256 * (k + 1)], ALU.add, ALU.add)
                v.then_inc(finished, 1)

            dve.wait_ge(cleared, 3)
            coefficients(0)
            for g in range(TGRP):
                copy_coef(0, 0, g)
            low_v(0, 0)
            for u in range(1, 4):
                low_v(0, u)
                centre(0, u - 1)
            low(0, 0)

            def step(i, r):
                s = r % STEPS
                if not beyond(i, r + 3):
                    centre(i, r + 3)
                if not beyond(i, r + 4):
                    low_v(i, r + 4)
                if not beyond(i, r + 1):
                    low(i, r + 1)
                if 1 <= s < 1 + TGRP and not beyond(i, r - s + STEPS):
                    copy_coef(tile_of(i, r) + 1, (r // STEPS + 1) % 2, s - 1)
                if not before(i, r, 1):
                    finish(i, r - 1)
                if s == 0 and not beyond(i, r + STEPS):
                    coefficients(tile_of(i, r) + 1)

            over_steps(dve, step)
            finish(ALL // PERIOD - 1, PERIOD - 1)


def kernel(x, L0_conv_weights1):
    import concourse.bacc as bacc
    from concourse.bass_utils import run_bass_kernel_spmd

    nc = bacc.Bacc("TRN2", target_bir_lowering=False, num_devices=1)
    arrays = {"x": np.ascontiguousarray(x), "weights": np.ascontiguousarray(L0_conv_weights1), **constants()}
    aps = {k: nc.dram_tensor(k, v.shape, mybir.dt.from_np(v.dtype), kind="ExternalInput").ap()
           for k, v in arrays.items()}
    out = nc.dram_tensor("out", (B, C, H, W), FP32, kind="ExternalOutput").ap()
    build(nc, aps["x"], aps["weights"], aps["mats"], aps["first"], aps["second"], out)
    r = run_bass_kernel_spmd(nc, [arrays], core_ids=[0])
    return r.results[0]["out"]
```

```python
from contextlib import ExitStack

import concourse.bass as bass
import concourse.mybir as mybir
import numpy as np

FP32 = mybir.dt.float32
FP32R = mybir.dt.float32r
ALU = mybir.AluOpType
ACT = mybir.ActivationFunctionType
AX = mybir.AxisListType

B, C, H, W = 32, 64, 128, 128
MODES = 20
NPIX = H * W
PLANES = B * C
TILE = 128
TILES = PLANES // TILE
CHUNK = 16
CHUNKS = TILE // CHUNK
NCHUNK = PLANES // CHUNK
SLOTS = 4
HALF = 8
NB = 2 * MODES + 1
MM = MODES * MODES
SPLIT = 12
OHALF = C // 2
WCH = 8
MGRP = 16
NW = OHALF // WCH
GROUPS = MM // MGRP
BGRP = 4
BATCHES = -(-GROUPS // BGRP)
DVE_SCALED = 9
WIDE = 4
PITCH = 64
TGRP = (NB + 3) // 4
STEPS = TILE // HALF
HI_ACT = 7
XSTEPS = SLOTS * CHUNK // HALF
EPS_NORM = 1e-5
EPS_SOBEL = 1e-8

SMALL = ["s1", "diffs", "s2", "mu", "tmp", "arg", "root", "scale", "new1", "new2", "isneg", "ms00", "m2",
         "xy", "var"]
MATS = ["flip", "flip2_neg", "flip_half", "flip2_neghalf", "smooth", "smooth_neg", "diff",
        "ident", "pair", "basis", "ones"]


def load_chunk(eng, buf, x_p, n, sem):
    for h in range(2):
        eng.dma_start(buf[:, HALF * h:HALF * (h + 1), :], x_p[:, bass.ds(n * CHUNK + HALF * h, HALF), :])\
            .then_inc(sem, 16)


def cos_index(j):
    return j


def sin_index(j):
    return MODES + j


def constants():
    n = np.arange(128)
    th = 2 * np.pi / 128
    jj = np.arange(MODES + 1)
    basis = np.concatenate([np.cos(th * np.outer(jj, n)), np.sin(th * np.outer(jj[1:], n))])
    m = {}
    flip = np.zeros((128, 128))
    flip[(-n) % 128, n] = 1
    flip2 = np.zeros((128, 128))
    flip2[(-n - 2) % 128, n] = 1
    m["flip"], m["flip2_neg"], m["flip_half"], m["flip2_neghalf"] = flip, -flip2, flip / 2, -flip2 / 2
    smooth = 2 * np.eye(128) + np.eye(128, k=1) + np.eye(128, k=-1)
    diff = np.eye(128, k=1) - np.eye(128, k=-1)
    m["smooth"], m["smooth_neg"], m["diff"] = smooth, -smooth, diff
    m["ident"], m["ones"] = np.eye(128), np.ones((128, 128))
    m["pair"] = np.kron(np.eye(64), np.ones((2, 2)))
    both = np.zeros((128, 128))
    both[0:NB] = basis
    both[64:64 + NB] = basis
    m["basis"] = both
    mats = np.stack([m[k] for k in MATS], 1)

    k2 = np.arange(MODES)
    w = n[:, None]
    second = np.zeros((128, NB, 3, MODES))
    for j in range(MODES + 1):
        late = th * (j + k2[None] * (w + 1))
        c, s = cos_index(j), sin_index(j)
        second[:, c, 0] = -np.sin(th * (k2[None] + 1) * w)
        second[:, c, 1] = np.cos(th * k2[None] * w) - np.sin(late)
        second[:, c, 2] = np.cos(th * k2[None] * w)
        if j:
            second[:, s, 0] = -np.cos(th * (k2[None] + 1) * w)
            second[:, s, 1] = -np.sin(th * k2[None] * w) - np.cos(late)
            second[:, s, 2] = -np.sin(th * k2[None] * w)
    return {"mats": mats.astype(np.float32), "first": np.pad(basis.T, ((0, 0), (0, PITCH - NB))).astype(np.float32),
            "second": second.reshape(128, NB, 3 * MODES).astype(np.float32)}


def build(nc, x, weights, mats_d, first_d, second_d, out):
    x_p = x.rearrange("b c h w -> h (b c) w")
    out_p = out.rearrange("b c h w -> h (b c) w")
    w_i = weights.rearrange("i o a b -> i o (a b)")

    keep = ExitStack()
    with keep:
        def sb(ctx, name, shape, dt=FP32):
            return ctx.enter_context(nc.sbuf_tensor(name, shape, dt))

        def ps(ctx, name, shape):
            words = int(np.prod(shape[1:]))
            flat = ctx.enter_context(nc.psum_tensor(name, [128, -(-words // 512) * 512], FP32))
            letters = "abcd"[:len(shape) - 1]
            sizes = dict(zip(letters, shape[1:]))
            return flat[:, 0:words].rearrange(f"p ({' '.join(letters)}) -> p {' '.join(letters)}", **sizes)

        def sem(name):
            return keep.enter_context(nc.semaphore(name))

        mats = sb(keep, "mats_sb", [128, len(MATS), 128])
        first = sb(keep, "first_sb", [128, PITCH])
        xbuf = sb(keep, "xbuf", [128, SLOTS, CHUNK, W])
        modes = sb(keep, "modes", [128, TILES, MM])
        rows = sb(keep, "rows", [128, 2, TILES, TILE])
        mean1 = sb(keep, "mean1", [128, TILES])
        corner = sb(keep, "corner", [128, TILES])
        mscale = sb(keep, "mscale", [128, 2, TILES])
        x_in = [sem(f"p2_x_in{s}") for s in range(XSTEPS)]

        def mat(name):
            return mats[:, MATS.index(name), :]

        mixing = ExitStack()
        with mixing:
            late = sb(mixing, "late", [128, TILES, MM])
            small = sb(mixing, "small", [128, len(SMALL), TILES])
            pass1(nc, sb, ps, sem, mat, x_p, mats, first, xbuf, modes, rows, late, small,
                  mats_d, first_d, second_d)
            mix(nc, sb, ps, sem, mat, w_i, x_p, xbuf, modes, rows, late, small, mean1, corner, mscale, x_in)
        pass2(nc, sb, ps, sem, mat, x_p, out_p, mats, xbuf, modes, rows, corner, mscale, x_in)


def x_of(xbuf, r):
    c, h = divmod(r, 2)
    return xbuf[:, c % SLOTS, HALF * h:HALF * (h + 1), :]


def load_step(eng, xbuf, x_p, u, slot, sem):
    eng.dma_start(x_of(xbuf, slot), x_p[:, bass.ds(u * HALF, HALF), :]).then_inc(sem, 16)


def pass1(nc, sb, ps, sem, mat, x_p, mats, first, xbuf, modes, rows, late, small, mats_d, first_d, second_d):
    ctx = ExitStack()
    with ctx:
        second = sb(ctx, "second_sb", [128, NB, 3 * MODES])
        tmodes = sb(ctx, "tmodes", [128, 2, NB, TILE])
        x_hi = sb(ctx, "m_hi", [128, 2, HALF, 64], FP32R)
        x_lo = sb(ctx, "m_lo", [128, 2, HALF, 64], FP32R)
        flips = sb(ctx, "flips", [128, 2, 128], FP32R)
        prod = sb(ctx, "prod", [128, 2, CHUNK, 64])
        edge = sb(ctx, "edge", [128, 2, TILE, 2, 2])
        edge_prod = sb(ctx, "edge_prod", [128, TILE, 2, 2])
        edge_sum = sb(ctx, "edge_sum", [128, TILE])
        square = sb(ctx, "square", [128, 2, HALF, W])
        t_ps = [ps(ctx, f"t_ps{g}", [128, HALF, PITCH]) for g in range(2)]
        z_ps = [ps(ctx, f"z_ps{g}", [128, 64, HALF]) for g in range(2)]
        edge_ps = ps(ctx, "edge_ps", [128, 2, TILE, 2])
        r_ps = [ps(ctx, f"r_ps{g}", [128, 512]) for g in range(2)]

        consts_in = sem("consts_in")
        second_in = sem("second_in")
        x_in = [sem(f"p1_x_in{s}") for s in range(SLOTS)]
        flips_ready = sem("p1_flips_ready")
        pe_first = sem("p1_pe_first")
        pe_mirror = sem("p1_pe_mirror")
        edge_in = sem("p1_edge_in")
        pe_edge = sem("p1_pe_edge")
        pe_second = sem("p1_pe_second")
        first_out = sem("p1_first_out")
        hi_ready = sem("p1_hi_ready")
        lo_ready = sem("p1_lo_ready")
        squared = sem("p1_squared")
        modes_out = sem("p1_modes_out")
        mirrored = sem("p1_mirrored")
        edge_muled = sem("p1_edge_muled")
        edge_summed = sem("p1_edge_summed")
        tile_done = sem("p1_tile_done")
        summed = sem("p1_summed")
        chunk_done = sem("p1_chunk_done")
        stats_pe = sem("p1_stats_pe")

        HALVES = 2 * CHUNKS
        block = ctx.enter_context(nc.Block())

        def over_tiles(eng, tile):
            tile(0, 0)
            with eng.Fori(0, TILES // 2 - 1) as j:
                tile(j * 2 + 1, 1)
                tile(j * 2 + 2, 0)
            tile(TILES - 1, 1)

        def is_first(i):
            return isinstance(i, int) and i == 0

        def arrived(i, k):
            return (i * (CHUNKS // SLOTS) + k // SLOTS + 1) * 32

        @block.sync
        def _(sp):
            load_chunk(sp, xbuf[:, 0], x_p, 0, x_in[0])
            sp.dma_start(mats[:], mats_d).then_inc(consts_in, 16)
            sp.dma_start(first[:], first_d).then_inc(consts_in, 16)
            for s in range(1, SLOTS):
                load_chunk(sp, xbuf[:, s], x_p, s, x_in[s])
            sp.dma_start(second[:], second_d).then_inc(second_in, 16)
            with sp.Fori(0, NCHUNK // SLOTS - 1) as j:
                for s in range(SLOTS):
                    sp.wait_ge(chunk_done, j * SLOTS + s + 1)
                    load_chunk(sp, xbuf[:, s], x_p, j * SLOTS + s + SLOTS, x_in[s])

        @block.gpsimd
        def _(pool):
            def tile(i, par):
                for k in range(CHUNKS):
                    for g in range(2):
                        pool.wait_ge(hi_ready, i * HALVES + 2 * k + g + 1)
                        nc.gpsimd.tensor_tensor(x_lo[:, g], xbuf[:, k % SLOTS, HALF * g:HALF * (g + 1), 64:],
                                                x_hi[:, g].bitcast(FP32), ALU.subtract).then_inc(lo_ready, 1)

            over_tiles(pool, tile)

        @block.tensor
        def _(pe):
            pe.wait_ge(consts_in, 32)
            pe.wait_ge(second_in, 16)
            pe.wait_ge(flips_ready, 2)
            pe.sem_inc(pe_second, 2)
            pe.sem_inc(pe_mirror, 2)

            per_chunk = -(-NB // (CHUNKS - 1))

            def second_axis(i, par, k):
                if k == 0:
                    pe.wait_ge(first_out, (i + 1) * HALVES + 2)
                    pe.wait_ge(modes_out, i + 1)
                edge = 2 * SPLIT
                for t in range(per_chunk * k, min(per_chunk * (k + 1), NB)):
                    j = t if t <= MODES else t - MODES
                    lo, hi = max(2 * j - 1, 0), min(2 * j + 2, 2 * MODES)
                    for bank, (a, b) in enumerate(((lo, min(hi, edge)), (max(lo, edge), hi))):
                        if a >= b:
                            continue
                        skip = a - (2 * j - 1)
                        mm = nc.tensor.matmul(
                            r_ps[bank][:, (a - edge * bank) * MODES:(b - edge * bank) * MODES],
                            tmodes[:, par, t, :], second[:, t, skip * MODES:(skip + b - a) * MODES],
                            start=t == (0, SPLIT)[bank], stop=t == NB - 1, skip_group_check=True)
                if k == CHUNKS - 2:
                    mm.then_inc(pe_second, 1)

            def edges(i, par):
                pe.wait_ge(edge_in, (i + 1) * CHUNKS)
                pe.wait_ge(edge_muled, i + 2)
                for a, flip in enumerate(("flip_half", "flip2_neghalf")):
                    mm = nc.tensor.matmul(edge_ps[:, a], mat(flip), edge[:, par, :, :, a],
                                          start=a == 0, stop=True, skip_group_check=True)
                mm.then_inc(pe_edge, 1)

            def tile(i, par):
                for k in range(CHUNKS):
                    slot = k % SLOTS
                    xs = xbuf[:, slot]
                    pe.wait_ge(x_in[slot], arrived(i, k))
                    for g in range(2):
                        pe.wait_ge(first_out, i * HALVES + 2 * k + g + 1)
                        for p in range(HALF):
                            mm = nc.tensor.matmul(t_ps[g][:, p, :], xs[:, HALF * g + p, :], first[:],
                                                  start=True, stop=True)
                        mm.then_inc(pe_first, 1)
                        if g and not is_first(i) and k < CHUNKS - 1:
                            second_axis(i - 1, 1 - par, k)
                        pe.wait_ge(mirrored, i * HALVES + 2 * k + g + 1)
                        pe.wait_ge(lo_ready, i * HALVES + 2 * k + g + 1)
                        for n, part in enumerate((x_hi, x_lo)):
                            rev = part[:, g, :, ::-1].rearrange("p n w -> p w n")
                            nc.tensor.matmul(z_ps[g][:, 1:64, :], flips[:, 0, :], rev[:, 0:63, :],
                                             start=n == 0, stop=False, skip_group_check=True)
                            mm = nc.tensor.matmul(z_ps[g][:, 0:63, :], flips[:, 1, :], rev[:, 1:64, :],
                                                  start=False, stop=n == 1, skip_group_check=True)
                        mm.then_inc(pe_mirror, 1)
                    if k == 1 and not is_first(i):
                        edges(i - 1, 1 - par)

            over_tiles(pe, tile)
            edges(TILES - 1, 1)
            pe.wait_ge(first_out, TILES * HALVES + 2)
            for t in range(TILES):
                if t == TILES - 1:
                    pe.wait_ge(tile_done, TILES)
                for a in range(2):
                    mm = nc.tensor.matmul(t_ps[0][:, a, t:t + 1], rows[:, a, t, :], mat("ones")[:, 0:1],
                                          start=True, stop=True, skip_group_check=True)
            mm.then_inc(stats_pe, 1)
            for k in range(CHUNKS - 1):
                second_axis(TILES - 1, 1, k)

        @block.scalar
        def _(act):
            act.sem_inc(first_out, 2)
            act.sem_inc(modes_out, 1)

            def high(i, k, g):
                act.wait_ge(x_in[k % SLOTS], arrived(i, k))
                act.wait_ge(pe_mirror, i * HALVES + 2 * k + g + 1)
                nc.scalar.activation(x_hi[:, g], xbuf[:, k % SLOTS, HALF * g:HALF * (g + 1), 64:],
                                     ACT.Copy).then_inc(hi_ready, 1)

            def copy_modes(i):
                act.wait_ge(pe_second, i + 3)
                na, nb = SPLIT, MODES - SPLIT
                for dst, which in ((modes, 0), (late, 1)):
                    d = dst[:, bass.ds(i, 1), :].rearrange("p t (a b) -> p (t a) b", b=MODES)
                    ra = r_ps[0][:, 0:na * 2 * MODES].rearrange("p (a v b) -> p a v b", v=2, b=MODES)
                    rb = r_ps[1][:, 0:nb * 2 * MODES].rearrange("p (a v b) -> p a v b", v=2, b=MODES)
                    nc.scalar.activation(d[:, 0:na, :], ra[:, :, which, :], ACT.Copy)
                    last = nc.scalar.activation(d[:, na:, :], rb[:, :, which, :], ACT.Copy)
                last.then_inc(modes_out, 1)

            def tile(i, par):
                act.wait_ge(pe_second, i + 1)
                act.wait_ge(edge_muled, i + 1)
                for k in range(CHUNKS):
                    for g in range(2):
                        high(i, k, g)
                        if g == 0:
                            nc.scalar.activation(edge[:, par, CHUNK * k:CHUNK * (k + 1)],
                                                 xbuf[:, k % SLOTS].rearrange("p n (b a) -> p n b a", b=2)
                                                 [:, :, :, 0:64:63], ACT.Copy).then_inc(edge_in, 1)
                        act.wait_ge(summed, i * HALVES + 2 * k + g + 1)
                        nc.scalar.activation(square[:, g], xbuf[:, k % SLOTS, HALF * g:HALF * (g + 1), :],
                                             ACT.Square).then_inc(squared, 1)
                        act.wait_ge(pe_first, i * HALVES + 2 * k + g + 1)
                        p0 = CHUNK * k + HALF * g
                        nc.scalar.activation(tmodes[:, par, :, p0:p0 + HALF].rearrange("w t p -> w p t"),
                                             t_ps[g][:, :, 0:NB], ACT.Copy).then_inc(first_out, 1)
                if not is_first(i):
                    copy_modes(i - 1)

            over_tiles(act, tile)
            copy_modes(TILES - 1)

        @block.vector
        def _(dve):
            dve.sem_inc(mirrored, 2)
            dve.sem_inc(edge_muled, 2)
            dve.sem_inc(summed, 2)
            dve.wait_ge(consts_in, 32)
            nc.vector.tensor_copy(flips[:, 0, :], mat("flip")).then_inc(flips_ready, 1)
            nc.vector.tensor_copy(flips[:, 1, :], mat("flip2_neg")).then_inc(flips_ready, 1)

            def edges(i, par):
                dve.wait_ge(pe_edge, i + 1)
                for a in range(2):
                    mul = nc.vector.tensor_tensor(edge_prod[:, :, :, a], edge[:, par, :, :, a],
                                                  edge_ps[:, a], ALU.mult)
                mul.then_inc(edge_muled, 1)
                dve.wait_ge(edge_muled, i + 3)
                nc.vector.tensor_reduce(edge_sum[:], edge_prod[:].rearrange("p n b a -> p n (b a)"),
                                        axis=AX.X, op=ALU.add).then_inc(edge_summed, 1)
                dve.wait_ge(edge_summed, i + 1)
                dve.wait_ge(chunk_done, (i + 1) * CHUNKS)
                row = rows[:, 0, bass.ds(i, 1), :]
                nc.vector.tensor_tensor(row, row, edge_sum[:].unsqueeze(1), ALU.add).then_inc(tile_done, 1)

            def tile(i, par):
                for k in range(CHUNKS):
                    slot = k % SLOTS
                    xs = xbuf[:, slot]
                    for g in range(2):
                        dve.wait_ge(squared, i * HALVES + 2 * k + g + 1)
                        p0 = CHUNK * k + HALF * g
                        nc.vector.tensor_reduce(rows[:, 1, bass.ds(i, 1), p0:p0 + HALF], square[:, g],
                                                axis=AX.X, op=ALU.add).then_inc(summed, 1)
                    for g in range(2):
                        dve.wait_ge(pe_mirror, i * HALVES + 2 * k + g + 3)
                        nc.vector.tensor_tensor(prod[:, k % 2, HALF * g:HALF * (g + 1), 0:64],
                                                xs[:, HALF * g:HALF * (g + 1), 0:64],
                                                z_ps[g].rearrange("p w n -> p n w"),
                                                ALU.mult).then_inc(mirrored, 1)
                    dve.wait_ge(mirrored, i * HALVES + 2 * k + 4)
                    nc.vector.tensor_reduce(rows[:, 0, bass.ds(i, 1), CHUNK * k:CHUNK * (k + 1)],
                                            prod[:, k % 2], axis=AX.X, op=ALU.add).then_inc(chunk_done, 1)
                    if k == 2 and not is_first(i):
                        edges(i - 1, 1 - par)

            over_tiles(dve, tile)
            edges(TILES - 1, 1)
            dve.wait_ge(stats_pe, 1)
            for a, name in enumerate(("diffs", "s2")):
                nc.vector.tensor_copy(small[:, SMALL.index(name), :], t_ps[0][:, a, 0:TILES])


def mirror_pieces():
    n = MODES
    return [((slice(0, 1), slice(0, 1)), (slice(0, 1), slice(0, 1))),
            ((slice(0, 1), slice(1, n)), (slice(0, 1), slice(n - 1, 0, -1))),
            ((slice(1, n), slice(0, 1)), (slice(n - 1, 0, -1), slice(0, 1))),
            ((slice(1, n), slice(1, n)), (slice(n - 1, 0, -1), slice(n - 1, 0, -1)))]


def mix(nc, sb, ps, sem, mat, w_i, x_p, xbuf, modes, rows, late, small, mean1, corner, mscale, x_in):
    ctx = ExitStack()
    with ctx:
        xmix = sb(ctx, "xmix", [128, TILES, 2, MM])
        wmix = sb(ctx, "wmix", [128, OHALF, MM])
        partial = sb(ctx, "partial", [128, 2, BATCHES, TILES])
        pair_ps = ps(ctx, "pair_ps", [128, 2, TILES])
        mix_ps = [ps(ctx, f"mix_ps{g}", [128, MGRP, B]) for g in range(4)]
        wide_ps = [ps(ctx, f"wide_ps{g}", [128, WIDE, 128]) for g in range(2)]

        chain = sem("m_chain")
        sums_ready = sem("m_sums_ready")
        paired = sem("m_paired")
        root_in = sem("m_root_in")
        rooted = sem("m_rooted")
        w_low_in = sem("m_w_low_in")
        w_raw_in = [sem(f"m_w_raw_in{s}") for s in range(2)]
        w_flipped = sem("m_w_flipped")
        scale_ready = sem("m_scale_ready")
        scaled = sem("m_scaled")
        act_scaled = sem("m_act_scaled")
        parted_dve = sem("m_parted_dve")
        parted_pool = sem("m_parted_pool")
        mixed = sem("m_mixed")
        act_out = sem("m_act_out")
        dve_out = sem("m_dve_out")
        m_squared = sem("m_m_squared")
        m_late = sem("m_m_late")
        reduced = sem("m_reduced")
        diag_ready = sem("m_diag_ready")
        widened = sem("m_widened")
        wide_out = sem("m_wide_out")

        raw = xbuf[:].rearrange("p s n w -> p s (n w)")
        batch_buf = rows[:].rearrange("p a t n -> p (a t n)").rearrange("p (a b n) -> p a b n", a=2, b=2)
        diag = xmix[:, 0:2, :, :].rearrange("p t q m -> p t (q m)")[:, :, 0:WIDE * 128]\
            .rearrange("p t (v n) -> p t v n", n=128)
        block = ctx.enter_context(nc.Block())

        def staged(s):
            return raw[C:128, 2 * s:2 * s + 2, :].rearrange("p s n -> p (s n)")[:, 0:WCH * MM]

        def mixed_pieces(n):
            c, g = divmod(n, GROUPS)
            src = mix_ps[n % 4][OHALF * c:OHALF * (c + 1)].rearrange("o m (t q) -> o q t m", q=2)
            for q in range(2):
                p = C * q + OHALF * c
                yield modes[p:p + OHALF, :, g * MGRP:(g + 1) * MGRP], src[:, q]

        def part(eng, upper, q):
            src = modes[C * q:C * (q + 1)].rearrange("p t (a b) -> p t a b", b=MODES)
            dst = xmix[C * upper:C * (upper + 1), :, q, :].rearrange("p t (a b) -> p t a b", b=MODES)
            for d, m in mirror_pieces():
                last = eng.tensor_tensor(dst[:, :, d[0], d[1]], src[:, :, d[0], d[1]], src[:, :, m[0], m[1]],
                                         (ALU.add, ALU.subtract)[upper])
            return last

        def batch(b):
            g1 = min(BGRP * (b + 1), GROUPS)
            return slice(BGRP * b * MGRP, g1 * MGRP), GROUPS + g1 - 1

        def batch_view(kind, b):
            m, _ = batch(b)
            n = m.stop - m.start
            return batch_buf[:, kind, b % 2, 0:TILES * n].rearrange("p (t m) -> p t m", m=n)

        @block.sync
        def _(sp):
            def raw_piece(n):
                if n >= 2:
                    sp.wait_ge(w_flipped, n - 1)
                sp.dma_start(staged(n % 2).rearrange("p (o m) -> p o m", m=MM),
                             w_i[:, n * WCH:(n + 1) * WCH, :]).then_inc(w_raw_in[n % 2], 16)

            def low_piece(n):
                q = n % NW
                sp.dma_start(wmix[0:C, q * WCH:(q + 1) * WCH], w_i[:, n * WCH:(n + 1) * WCH, :])\
                    .then_inc(w_low_in, 16)

            for n in range(NW):
                raw_piece(n)
                low_piece(n)
            raw_piece(NW)
            raw_piece(NW + 1)
            sp.wait_ge(mixed, GROUPS)
            for n in range(NW, 2 * NW):
                if n >= NW + 2:
                    raw_piece(n)
                low_piece(n)
            sp.wait_ge(w_flipped, 2 * NW)
            for slot in range(XSTEPS):
                load_step(sp, xbuf, x_p, slot, slot, x_in[slot])

        @block.gpsimd
        def _(pool):
            pool.wait_ge(scaled, 1)
            pool.wait_ge(act_scaled, 1)
            part(nc.gpsimd, 1, 0).then_inc(parted_pool, 1)
            for b in range(BATCHES):
                m, last = batch(b)
                pool.wait_ge(act_out, last // 2 + 1)
                pool.wait_ge(dve_out, (last + 1) // 2)
                if b >= 2:
                    pool.wait_ge(reduced, b - 1)
                nc.gpsimd.tensor_tensor(batch_view(1, b), modes[:, :, m], late[:, :, m], ALU.mult)\
                    .then_inc(m_late, 1)

        @block.tensor
        def _(pe):
            pe.wait_ge(sums_ready, 1)
            nc.tensor.matmul(pair_ps[:, 0, :], mat("pair"), small[:, SMALL.index("s1"), :],
                             start=True, stop=True).then_inc(paired, 1)
            pe.wait_ge(parted_dve, 1)
            pe.wait_ge(parted_pool, 1)
            for c in range(2):
                pe.wait_ge(w_low_in, (c + 1) * NW * 16)
                pe.wait_ge(w_flipped, (c + 1) * NW)
                for g in range(GROUPS):
                    n = c * GROUPS + g
                    if n >= 4:
                        pe.wait_ge(act_out if n % 2 == 0 else dve_out, n // 2 - 1)
                    for m in range(MGRP):
                        k = g * MGRP + m
                        mm = nc.tensor.matmul(mix_ps[n % 4][OHALF * c:OHALF * (c + 1), m, :],
                                              wmix[:, :, k], xmix[:].rearrange("p t q m -> p (t q) m")[:, :, k],
                                              start=True, stop=True)
                    mm.then_inc(mixed, 1)
            pe.wait_ge(sums_ready, 2)
            n1 = SMALL.index("new1")
            nc.tensor.matmul(pair_ps[:].rearrange("p a t -> p (a t)"), mat("pair"),
                             small[:, n1:n1 + 2, :].rearrange("p a t -> p (a t)"), start=True, stop=True)\
                .then_inc(paired, 1)
            for n in range(2 * TILES // WIDE):
                pe.wait_ge(diag_ready, n + 1)
                if n >= 2:
                    pe.wait_ge(wide_out, n - 1)
                nc.tensor.matmul(wide_ps[n % 2][:], mat("ones"), diag[:, n % 2],
                                 start=True, stop=True).then_inc(widened, 1)

        @block.scalar
        def _(act):
            arg, root, scale = (small[:, SMALL.index(n), :] for n in ("arg", "root", "scale"))

            def mirror_weights(n):
                act.wait_ge(w_raw_in[n % 2], 16 * (n // 2 + 1))
                q = n % NW
                dst = wmix[C:128, q * WCH:(q + 1) * WCH, :].rearrange("p o (a b) -> p o a b", b=MODES)
                src = staged(n % 2).rearrange("p (o a b) -> p o a b", a=MODES, b=MODES)
                for d, s in mirror_pieces():
                    cp = nc.scalar.activation(dst[:, :, d[0], d[1]], src[:, :, s[0], s[1]], ACT.Copy)
                cp.then_inc(w_flipped, 1)

            act.wait_ge(root_in, 1)
            nc.scalar.activation(root, arg, ACT.Sqrt, scale=4.0 * NPIX).then_inc(rooted, 1)
            act.wait_ge(scale_ready, 1)
            for t in range(DVE_SCALED, TILES):
                scaling = nc.scalar.activation(modes[:, t, :], modes[:, t, :], ACT.Copy, scale=scale[:, t:t + 1])
            scaling.then_inc(act_scaled, 1)
            for n in range(NW):
                mirror_weights(n)
            act.wait_ge(parted_dve, 1)
            act.wait_ge(parted_pool, 1)
            for n in range(0, 2 * GROUPS, 2):
                if n == GROUPS + 1:
                    act.wait_ge(mixed, GROUPS)
                    for piece in range(NW, 2 * NW):
                        mirror_weights(piece)
                act.wait_ge(mixed, n + 1)
                for dst, src in mixed_pieces(n):
                    cp = nc.scalar.activation(dst, src, ACT.Copy)
                cp.then_inc(act_out, 1)
                for b in range(BATCHES):
                    m, last = batch(b)
                    if last // 2 * 2 != n:
                        continue
                    act.wait_ge(act_out, n // 2 + 1)
                    act.wait_ge(dve_out, (last + 1) // 2)
                    if b >= 2:
                        act.wait_ge(reduced, b - 1)
                    nc.scalar.activation(batch_view(0, b), modes[:, :, m], ACT.Square).then_inc(m_squared, 1)
            act.wait_ge(root_in, 2)
            nc.scalar.activation(root, arg, ACT.Sqrt, scale=float(NPIX) ** 3).then_inc(rooted, 1)
            for n in range(2 * TILES // WIDE):
                act.wait_ge(widened, n + 1)
                t0 = n * WIDE % TILES
                nc.scalar.activation(rows[:, n * WIDE // TILES, t0:t0 + WIDE, :], wide_ps[n % 2][:],
                                     ACT.Copy).then_inc(wide_out, 1)

        @block.vector
        def _(dve):
            done = [0]

            def link(ins):
                done[0] += 1
                ins.then_inc(chain, 1)
                dve.wait_ge(chain, done[0])

            V = nc.vector
            s1, diffs, s2, mu, tmp, arg, root, scale, new1, new2, isneg, ms00, m2, xy, var = (
                small[:, n, :] for n in range(len(SMALL)))

            link(V.tensor_copy(s1, modes[:, :, 0]))
            dve.sem_inc(sums_ready, 1)
            dve.wait_ge(paired, 1)
            link(V.tensor_scalar(mu, pair_ps[:, 0, :], 1.0 / (2 * NPIX), None, ALU.mult))
            link(V.scalar_tensor_tensor(modes[:, :, 0], mu, -float(NPIX), s1, ALU.mult, ALU.add))
            link(V.tensor_tensor(arg, s1, modes[:, :, 0], ALU.add))
            link(V.tensor_tensor(arg, arg, mu, ALU.mult))
            link(V.tensor_tensor(arg, s2, arg, ALU.subtract))
            link(V.tensor_tensor(arg, arg, diffs, ALU.add))

            def inverse_root(n):
                link(V.tensor_scalar(isneg, arg, 0.0, None, ALU.is_le))
                V.tensor_tensor(arg, arg, isneg, ALU.max).then_inc(root_in, 1)
                dve.wait_ge(rooted, n)
                link(V.reciprocal(scale, root))
                link(V.tensor_scalar(isneg, isneg, -1.0, 1.0, ALU.mult, ALU.add))
                link(V.tensor_tensor(scale, scale, isneg, ALU.mult))

            inverse_root(1)
            dve.sem_inc(scale_ready, 1)
            m = modes[:, 0:DVE_SCALED]
            V.tensor_tensor(m, m, scale[:, 0:DVE_SCALED].unsqueeze(2).to_broadcast([128, DVE_SCALED, MM]), ALU.mult)\
                .then_inc(scaled, 1)
            dve.wait_ge(scaled, 1)
            dve.wait_ge(act_scaled, 1)
            part(V, 0, 0)
            part(V, 0, 1)
            part(V, 1, 1).then_inc(parted_dve, 1)
            dve.wait_ge(parted_pool, 1)
            dve.wait_ge(parted_dve, 1)

            def reduce_batch(b):
                dve.wait_ge(m_squared, b + 1)
                V.tensor_reduce(partial[:, 0, b, :], batch_view(0, b), axis=AX.X, op=ALU.add)
                dve.wait_ge(m_late, b + 1)
                V.tensor_reduce(partial[:, 1, b, :], batch_view(1, b), axis=AX.X, op=ALU.add)\
                    .then_inc(reduced, 1)

            todo = 0
            for n in range(1, 2 * GROUPS, 2):
                dve.wait_ge(mixed, n + 1)
                for dst, src in mixed_pieces(n):
                    cp = V.tensor_copy(dst, src)
                cp.then_inc(dve_out, 1)
                if todo < BATCHES and n >= batch(todo)[1] + 3:
                    reduce_batch(todo)
                    todo += 1
            for b in range(todo, BATCHES):
                reduce_batch(b)
            dve.wait_ge(reduced, BATCHES)
            link(V.tensor_tensor(tmp, modes[:, :, 0], modes[:, :, 0], ALU.mult))
            link(V.tensor_reduce(m2, partial[:, 0].rearrange("p b t -> p t b"), axis=AX.X, op=ALU.add))
            link(V.tensor_reduce(xy, partial[:, 1].rearrange("p b t -> p t b"), axis=AX.X, op=ALU.add))
            link(V.scalar_tensor_tensor(m2, tmp, 0.5, m2, ALU.mult, ALU.add))
            link(V.tensor_copy(arg, m2))
            inverse_root(2)
            V.tensor_copy(mscale[:, 0, :], scale)
            V.tensor_scalar(mscale[:, 1, :], scale, -1.0, None, ALU.mult)
            link(V.tensor_tensor(ms00, modes[:, :, 0], scale, ALU.mult))
            link(V.tensor_tensor(xy, xy, scale, ALU.mult))
            link(V.scalar_tensor_tensor(new1, ms00, float(NPIX), s1, ALU.mult, ALU.add))
            link(V.tensor_tensor(m2, m2, scale, ALU.mult))
            link(V.tensor_tensor(m2, m2, scale, ALU.mult))
            link(V.scalar_tensor_tensor(new2, xy, 2.0, s2, ALU.mult, ALU.add))
            link(V.scalar_tensor_tensor(new2, m2, float(NPIX), new2, ALU.mult, ALU.add))
            dve.sem_inc(sums_ready, 1)
            dve.wait_ge(paired, 2)
            link(V.tensor_scalar(mean1[:], pair_ps[:, 0, :], 1.0 / (2 * NPIX), None, ALU.mult))
            link(V.tensor_tensor(tmp, mean1[:], mean1[:], ALU.mult))
            link(V.scalar_tensor_tensor(var, pair_ps[:, 1, :], 1.0 / (2 * NPIX), tmp, ALU.mult, ALU.subtract))
            link(V.tensor_scalar(var, var, 0.0, EPS_NORM, ALU.max, ALU.add))
            link(V.reciprocal(var, var))
            link(V.tensor_tensor(corner[:], ms00, mean1[:], ALU.subtract))
            for n in range(2 * TILES // WIDE):
                t0 = n * WIDE % TILES
                value = (var if n * WIDE < TILES else mean1[:])[:, t0:t0 + WIDE]
                if n >= 2:
                    dve.wait_ge(widened, n - 1)
                V.tensor_tensor(diag[:, n % 2], mat("ident").unsqueeze(1).to_broadcast([128, WIDE, 128]),
                                value.unsqueeze(2).to_broadcast([128, WIDE, 128]), ALU.mult)\
                    .then_inc(diag_ready, 1)


def pass2(nc, sb, ps, sem, mat, x_p, out_p, mats, xbuf, modes, rows, corner, mscale, x_in):
    ctx = ExitStack()
    with ctx:
        coef_flat = sb(ctx, "coef", [128, NB * NB + 128])
        coef = coef_flat[:, 0:NB * NB].rearrange("p (a b) -> p a b", b=NB)
        coef_t = sb(ctx, "coef_t", [NB, 2, TILE, PITCH])
        v_sb = sb(ctx, "v_sb", [128, 2, 2, HALF // 2, W], FP32R)
        basis = sb(ctx, "basis", [128, 2, 128], FP32R)
        pairs = sb(ctx, "pairs", [128, 2, HALF, W + 2])
        p_hi = sb(ctx, "p_hi", [128, 2, HALF, W + 2], FP32R)
        p_lo = sb(ctx, "p_lo", [128, 2, HALF, W + 2], FP32R)
        stencil = sb(ctx, "stencil", [128, 3, 128], FP32R)
        grad = sb(ctx, "grad", [128, 2, 2, 2, 512])
        eps = sb(ctx, "eps", [128, 1])
        v_ps = ps(ctx, "v_ps", [128, HALF // 2, W])
        t_ps = ps(ctx, "t_ps", [128, 4, TILE])
        y_ps = ps(ctx, "y_ps", [128, 2, HALF // 2, W])
        g_ps = [ps(ctx, f"g_ps{h}", [128, 2, 4, W]) for h in range(2)]
        tile0_ps = [t_ps, g_ps[0][:, 0], g_ps[0][:, 1], g_ps[1][:, 0], g_ps[1][:, 1], y_ps[:, 0]]

        stored = [sem(f"p2_stored{s}") for s in range(XSTEPS)]
        setup = sem("p2_setup")
        cleared = sem("p2_cleared")
        coef_zero = sem("p2_coef_zero")
        tile0_out = sem("p2_tile0_out")
        tile0_act = sem("p2_tile0_act")
        basis_hi = sem("p2_basis_hi")
        coef_main = sem("p2_coef_main")
        coef_ready = sem("p2_coef_ready")
        pe_t = sem("p2_pe_t")
        coef_out = sem("p2_coef_out")
        pe_v = sem("p2_pe_v")
        v_hi = sem("p2_v_hi")
        v_out = sem("p2_v_out")
        pe_y = sem("p2_pe_y")
        centred = sem("p2_centred")
        pairs_ready = sem("p2_pairs_ready")
        hi_ready = sem("p2_hi_ready")
        pool_hi = sem("p2_pool_hi")
        lo_ready = sem("p2_lo_ready")
        pe_grad = sem("p2_pe_grad")
        squared = sem("p2_squared")
        added = sem("p2_added")
        rooted = sem("p2_rooted")
        finished = sem("p2_finished")

        PERIOD = 2 * STEPS
        ALL = TILES * STEPS
        block = ctx.enter_context(nc.Block())

        def over_steps(eng, step):
            step(0, 0)
            with eng.Fori(0, ALL // PERIOD - 1) as i:
                for r in range(1, PERIOD + 1):
                    step(i, r)
            for r in range(1, PERIOD):
                step(ALL // PERIOD - 1, r)

        def at(i, r):
            return i * PERIOD + r

        def before(i, r, n):
            return isinstance(i, int) and at(i, r) < n

        def beyond(i, r):
            return isinstance(i, int) and at(i, r) >= ALL

        def tile_of(i, r):
            return i * (PERIOD // STEPS) + r // STEPS

        def first_plane(i, r):
            return at(i, r) * HALF

        @block.sync
        def _(sp):
            def store(u0, slot):
                done = sp.snap(u0 + slot + 2)
                plane = sp.snap((u0 + slot) * HALF)
                sp.wait_ge(finished, done)
                sp.dma_start(out_p[:, bass.ds(plane, HALF), :], x_of(xbuf, slot)).then_inc(stored[slot], 16)

            with sp.Fori(0, ALL // XSTEPS - 1) as j:
                for slot in range(XSTEPS):
                    store(j * XSTEPS, slot)
                    count = sp.snap((j + 1) * 16)
                    after = sp.snap((j + 1) * XSTEPS + slot)
                    sp.wait_ge(stored[slot], count)
                    load_step(sp, xbuf, x_p, after, slot, x_in[slot])
            for slot in range(XSTEPS):
                store(ALL - XSTEPS, slot)
            for slot in range(XSTEPS):
                sp.wait_ge(stored[slot], ALL // XSTEPS * 16)

        @block.gpsimd
        def _(pool):
            for par in range(2):
                nc.gpsimd.memset(coef_t[:, par, :, NB:PITCH], 0.0).then_inc(cleared, 1)

            def neighbours(i, r):
                pool.wait_ge(centred, at(i, r) + 1)
                if not before(i, r, 2):
                    pool.wait_ge(lo_ready, at(i, r) - 1)
                u, q = x_of(xbuf, r), pairs[:, r % 2]
                nc.gpsimd.tensor_tensor(q[:, :, 1:W], u[:, :, 0:W - 1], u[:, :, 1:W], ALU.add)
                nc.gpsimd.tensor_copy(q[:, :, 0:W + 1:W], u[:, :, 0:W:W - 1]).then_inc(pairs_ready, 1)

            def high(i, r):
                if not before(i, r, 2):
                    pool.wait_ge(pe_grad, at(i, r) * 2 - 2)
                u, q = x_of(xbuf, r)[:, HI_ACT:], p_hi[:, r % 2, HI_ACT:]
                nc.gpsimd.tensor_tensor(q[:, :, 1:W], u[:, :, 0:W - 1], u[:, :, 1:W], ALU.add)
                nc.gpsimd.tensor_copy(q[:, :, 0:W + 1:W], u[:, :, 0:W:W - 1]).then_inc(pool_hi, 1)

            def add(i, r, h):
                pool.wait_ge(squared, at(i, r) * 2 + h + 1)
                f = grad[:, r % 2, h]
                nc.gpsimd.tensor_tensor(f[:, 0], f[:, 0], f[:, 1], ALU.add).then_inc(added, 1)

            def step(i, r):
                if not before(i, r, 1):
                    add(i, r - 1, 0)
                if not beyond(i, r + 1):
                    high(i, r + 1)
                if not before(i, r, 1):
                    add(i, r - 1, 1)
                if not beyond(i, r + 2):
                    neighbours(i, r + 2)

            neighbours(0, 0)
            neighbours(0, 1)
            high(0, 0)
            over_steps(pool, step)
            for h in range(2):
                add(ALL // PERIOD - 1, PERIOD - 1, h)

        @block.tensor
        def _(pe):
            def transposes(t, par, g, buf=t_ps):
                if g == 0:
                    pe.wait_ge(coef_ready, t + 1)
                if not (isinstance(t, int) and t == 0):
                    pe.wait_ge(coef_out, t * TGRP + g)
                for j in range(4 * g, min(4 * g + 4, NB)):
                    mm = nc.tensor.transpose(buf[:, j - 4 * g, :], coef_flat[:, NB * j:NB * j + 128], mat("ident"))
                mm.then_inc(pe_t, 1)

            def second_axis(i, r):
                if r % STEPS == 0:
                    pe.wait_ge(coef_out, (tile_of(i, r) + 1) * TGRP)
                if not before(i, r, 1):
                    pe.wait_ge(v_out, at(i, r))
                p0 = (r % STEPS) * HALF
                for q in range(HALF // 2):
                    mm = nc.tensor.matmul(
                        v_ps[:, q, :],
                        coef_t[0:NB, r // STEPS % 2, p0 + 2 * q:p0 + 2 * q + 2, :].rearrange("k p j -> k (p j)"),
                        mat("basis")[0:NB, :], start=True, stop=True)
                mm.then_inc(pe_v, 1)

            def first_axis(i, r):
                pe.wait_ge(v_out, at(i, r) + 1)
                if not before(i, r, 1):
                    pe.wait_ge(centred, at(i, r))
                for q in range(2):
                    for n in range(2):
                        mm = nc.tensor.matmul(y_ps[:, q], basis[:, n, :], v_sb[:, r % 2, q],
                                              start=n == 0, stop=n == 1)
                mm.then_inc(pe_y, 1)

            def sobel(i, r):
                pe.wait_ge(lo_ready, at(i, r) + 1)
                SMOOTH, SMOOTH_NEG, DIFF = range(3)
                taps = [(0, SMOOTH_NEG, 0), (0, SMOOTH, 1), (1, DIFF, 0), (1, DIFF, 1)]
                for h in range(2):
                    if not before(i, r, 1):
                        pe.wait_ge(squared, at(i, r) * 2 + h - 1)
                    for axis in range(2):
                        todo = [(x, m, o) for a, m, o in taps if a == axis for x in (p_hi, p_lo)]
                        for n, (x, m, o) in enumerate(todo):
                            mm = nc.tensor.matmul(g_ps[h][:, axis], stencil[:, m, :],
                                                  x[:, r % 2, 4 * h:4 * h + 4, o:o + W],
                                                  start=n == 0, stop=n == len(todo) - 1)
                    mm.then_inc(pe_grad, 1)

            for g in range(TGRP):
                if g >= len(tile0_ps):
                    pe.wait_ge((tile0_out, tile0_act)[g % 2], (g - len(tile0_ps)) // 2 + 1)
                transposes(0, 0, g, tile0_ps[g % len(tile0_ps)])
            second_axis(0, 0)
            second_axis(0, 1)
            pe.wait_ge(setup, 1)
            first_axis(0, 0)
            for u in range(2, 4):
                second_axis(0, u)
                first_axis(0, u - 1)

            def step(i, r):
                s = r % STEPS
                if not beyond(i, r + 4):
                    second_axis(i, r + 4)
                if not beyond(i, r + 3):
                    first_axis(i, r + 3)
                if s < TGRP and not beyond(i, r - s + STEPS):
                    transposes(tile_of(i, r) + 1, (r // STEPS + 1) % 2, s)
                sobel(i, r)

            over_steps(pe, step)

        @block.scalar
        def _(act):
            def high(i, r):
                act.wait_ge(pairs_ready, at(i, r) + 1)
                if not before(i, r, 2):
                    act.wait_ge(pe_grad, at(i, r) * 2 - 2)
                n = HI_ACT
                nc.scalar.activation(p_hi[:, r % 2, 0:n, 0:W + 1], pairs[:, r % 2, 0:n, 0:W + 1], ACT.Copy)\
                    .then_inc(hi_ready, 1)

            def copy_v(i, r):
                act.wait_ge(pe_v, at(i, r) + 1)
                if not before(i, r, 2):
                    act.wait_ge(pe_y, at(i, r) - 1)
                for q in range(2):
                    v = nc.scalar.activation(v_sb[0:64, r % 2, q], v_ps[64 * q:64 * (q + 1)], ACT.Copy)
                v.then_inc(v_hi, 1)

            def squares(i, r, h):
                act.wait_ge(pe_grad, at(i, r) * 2 + h + 1)
                if not before(i, r, 2):
                    act.wait_ge(finished, at(i, r))
                nc.scalar.activation(grad[:, r % 2, h], g_ps[h][:].rearrange("p a n w -> p a (n w)"),
                                     ACT.Square).then_inc(squared, 1)

            def roots(i, r, h):
                act.wait_ge(added, at(i, r) * 2 + h + 1)
                inv_var = rows[:, 0].rearrange("p t n -> p (t n)")
                for k in range(2):
                    f = grad[:, r % 2, h, 0, 256 * k:256 * (k + 1)]
                    a = nc.scalar.activation(f, f, ACT.Sqrt, bias=eps[:],
                                             scale=inv_var[:, bass.ds(first_plane(i, r) + 4 * h + 2 * k, 1)])
                a.then_inc(rooted, 1)

            for g in range(1, TGRP, 2):
                act.wait_ge(pe_t, g + 1)
                n = min(4, NB - 4 * g)
                nc.scalar.activation(coef_t[:, 0, :, 4 * g:4 * g + n].rearrange("k p j -> k j p"),
                                     tile0_ps[g % len(tile0_ps)][0:NB, 0:n, :], ACT.Copy).then_inc(tile0_act, 1)
            act.wait_ge(setup, 1)
            for u in range(4):
                copy_v(0, u)
            high(0, 0)

            def step(i, r):
                if not beyond(i, r + 4):
                    copy_v(i, r + 4)
                if not before(i, r, 1):
                    roots(i, r - 1, 0)
                if not beyond(i, r + 1):
                    high(i, r + 1)
                if not before(i, r, 1):
                    roots(i, r - 1, 1)
                squares(i, r, 0)
                squares(i, r, 1)

            over_steps(act, step)
            roots(ALL // PERIOD - 1, PERIOD - 1, 0)
            roots(ALL // PERIOD - 1, PERIOD - 1, 1)

        @block.vector
        def _(dve):
            V = nc.vector
            dve.sem_inc(finished, 1)

            def copy_coef(t, par, g):
                n = min(4, NB - 4 * g)
                dve.wait_ge(pe_t, t * TGRP + g + 1)
                V.tensor_copy(coef_t[:, par, :, 4 * g:4 * g + n].rearrange("k p j -> k j p"),
                              t_ps[0:NB, 0:n, :]).then_inc(coef_out, 1)

            def centre(i, r):
                dve.wait_ge(pe_y, at(i, r) + 1)
                dve.wait_ge(x_in[r % XSTEPS], (i * (PERIOD // XSTEPS) + r // XSTEPS + 1) * 16)
                xs = x_of(xbuf, r).rearrange("p (k q) w -> p q k w", q=2)
                V.tensor_tensor(xs, xs, y_ps[:], ALU.add).then_inc(centred, 1)

            def low(i, r):
                dve.wait_ge(hi_ready, at(i, r) + 1)
                dve.wait_ge(pool_hi, at(i, r) + 1)
                if not before(i, r, 2):
                    dve.wait_ge(pe_grad, at(i, r) * 2 - 2)
                V.tensor_tensor(p_lo[:, r % 2, :, 0:W + 1], pairs[:, r % 2, :, 0:W + 1],
                                p_hi[:, r % 2, :, 0:W + 1].bitcast(FP32), ALU.subtract).then_inc(lo_ready, 1)

            def low_v(i, r):
                dve.wait_ge(v_hi, at(i, r) + 1)
                for q in range(2):
                    v = V.tensor_tensor(v_sb[64:128, r % 2, q], v_ps[64 * q:64 * (q + 1)],
                                        v_sb[0:64, r % 2, q].bitcast(FP32), ALU.subtract)
                v.then_inc(v_out, 1)

            def coefficients(t, part):
                n = MODES
                m = modes[:, bass.ds(t, 1), :].rearrange("p t (a b) -> p (t a) b", b=n)
                c0, c1, s1 = slice(0, n), slice(1, n + 1), slice(n + 1, 2 * n + 1)
                plus, minus = (mscale[:, a, bass.ds(t, 1)] for a in range(2))
                if part == 0:
                    V.tensor_scalar(coef[:, c0, c0], m, plus, None, ALU.mult).then_inc(coef_main, 1)
                elif part == 1:
                    V.tensor_scalar(coef[:, n + 1:2 * n, n + 1:2 * n], m[:, 1:, 1:], minus, None, ALU.mult)
                elif part == 2:
                    V.tensor_scalar(coef[:, s1, c1], m, minus, None, ALU.mult)
                else:
                    V.tensor_scalar(coef[:, c1, s1], m, minus, None, ALU.mult)
                    dve.wait_ge(coef_main, t + 1)
                    V.tensor_copy(coef[:, 0, 0:1], corner[:, bass.ds(t, 1)]).then_inc(coef_ready, 1)

            def finish(i, r):
                mean = rows[:, 1].rearrange("p t n -> p (t n)")
                for h in range(2):
                    dve.wait_ge(rooted, at(i, r) * 2 + h + 1)
                    for k in range(2):
                        xs = x_of(xbuf, r)[:, 4 * h + 2 * k:4 * h + 2 * k + 2, :].rearrange("p n w -> p (n w)")
                        v = V.scalar_tensor_tensor(
                            xs, xs, mean[:, bass.ds(first_plane(i, r) + 4 * h + 2 * k, 1)],
                            grad[:, r % 2, h, 0, 256 * k:256 * (k + 1)], ALU.add, ALU.add)
                v.then_inc(finished, 1)

            V.memset(coef_flat[:], 0.0).then_inc(coef_zero, 1)
            dve.wait_ge(coef_zero, 1)
            for part in range(4):
                coefficients(0, part)
            for n, m in enumerate(("smooth", "smooth_neg", "diff")):
                V.tensor_copy(stencil[:, n, :], mat(m))
            V.tensor_copy(basis[:, 0, :], mat("basis")).then_inc(basis_hi, 1)
            dve.wait_ge(basis_hi, 1)
            V.tensor_tensor(basis[:, 1, :], mat("basis"), basis[:, 0, :].bitcast(FP32), ALU.subtract)
            V.memset(eps[:], EPS_SOBEL).then_inc(setup, 1)
            for g in range(0, TGRP, 2):
                dve.wait_ge(pe_t, g + 1)
                n = min(4, NB - 4 * g)
                V.tensor_copy(coef_t[:, 0, :, 4 * g:4 * g + n].rearrange("k p j -> k j p"),
                              tile0_ps[g % len(tile0_ps)][0:NB, 0:n, :]).then_inc(tile0_out, 1)
            dve.wait_ge(cleared, 2)
            dve.wait_ge(tile0_act, TGRP // 2)
            dve.wait_ge(tile0_out, TGRP - TGRP // 2)
            dve.sem_inc(coef_out, TGRP)
            for part in range(4):
                coefficients(1, part)
            low_v(0, 0)
            for u in range(1, 4):
                low_v(0, u)
                centre(0, u - 1)
            low(0, 0)

            def step(i, r):
                s = r % STEPS
                if not beyond(i, r + 3):
                    centre(i, r + 3)
                if not beyond(i, r + 4):
                    low_v(i, r + 4)
                if not beyond(i, r + 1):
                    low(i, r + 1)
                if s < TGRP and not beyond(i, r - s + STEPS):
                    copy_coef(tile_of(i, r) + 1, (r // STEPS + 1) % 2, s)
                if 0 <= s - TGRP < 4 and not beyond(i, r - s + 2 * STEPS):
                    coefficients(tile_of(i, r) + 2, s - TGRP)
                if not before(i, r, 1):
                    finish(i, r - 1)

            over_steps(dve, step)
            finish(ALL // PERIOD - 1, PERIOD - 1)


def kernel(x, L0_conv_weights1):
    import concourse.bacc as bacc
    from concourse.bass_utils import run_bass_kernel_spmd

    nc = bacc.Bacc("TRN2", target_bir_lowering=False, num_devices=1)
    arrays = {"x": np.ascontiguousarray(x), "weights": np.ascontiguousarray(L0_conv_weights1), **constants()}
    aps = {k: nc.dram_tensor(k, v.shape, mybir.dt.from_np(v.dtype), kind="ExternalInput").ap()
           for k, v in arrays.items()}
    out = nc.dram_tensor("out", (B, C, H, W), FP32, kind="ExternalOutput").ap()
    build(nc, aps["x"], aps["weights"], aps["mats"], aps["first"], aps["second"], out)
    r = run_bass_kernel_spmd(nc, [arrays], core_ids=[0])
    return r.results[0]["out"]
```
